# Optimizing a Trainium2 kernel written in Bass

```python
import numpy as np
import jax
import jax.numpy as jnp

def _softmax(x, axis=-1):
    return jax.nn.softmax(x, axis=axis)

def _gelu(x):
    return jax.nn.gelu(x, approximate=True)

def _silu(x):
    return jax.nn.silu(x)

def _sigmoid(x):
    return jax.nn.sigmoid(x)

def _layernorm(x, axis=-1, eps=1e-05):
    m = jnp.mean(x, axis=axis, keepdims=True)
    v = jnp.var(x, axis=axis, keepdims=True)
    return (x - m) / jnp.sqrt(v + eps)

def _scatter_add(tgt, idx, src, axis=0):
    return tgt.at[idx].add(src)

def _segment_sum(src, seg, n):
    return jax.ops.segment_sum(src, seg, n)
kernel_name = 'mk_seq_preln_d1_jaxref_r4_1f2186'

def setup_inputs(seed: int=0):
    np.random.seed(seed)
    _w = jnp.asarray

    def _L0_attn_setup():
        import jax, jax.numpy as jnp
        import numpy as np
        D_INNER, D_STATE, DT_RANK = (512, 16, 128)
        BATCH, SEQ = (2, 512)

        def _selective_scan(u, delta, A, B, C, D):
            dA = jnp.exp(delta[..., None] * A[None, None])
            dBu = (delta * u)[..., None] * B[:, :, None, :]

            def step(h, inp):
                dA_t, dBu_t, C_t = inp
                h = dA_t * h + dBu_t
                y_t = jnp.einsum('bdn,bn->bd', h, C_t)
                return (h, y_t)
            h0 = jnp.zeros((u.shape[0], u.shape[2], A.shape[1]), dtype=u.dtype)
            xs = (jnp.moveaxis(dA, 1, 0), jnp.moveaxis(dBu, 1, 0), jnp.moveaxis(C, 1, 0))
            _, ys = jax.lax.scan(step, h0, xs)
            y = jnp.moveaxis(ys, 0, 1)
            return y + u * D[None, None, :]
        key = jax.random.key(seed)
        ks = jax.random.split(key, 6)
        x = jax.random.normal(ks[0], (BATCH, SEQ, D_INNER), dtype=jnp.float32)
        A_log = jax.random.uniform(ks[1], (D_INNER, D_STATE), minval=-4.0, maxval=-1.0, dtype=jnp.float32)
        D = jnp.ones((D_INNER,), dtype=jnp.float32)
        x_proj_w = jax.random.normal(ks[2], (DT_RANK + 2 * D_STATE, D_INNER), dtype=jnp.float32) / np.sqrt(D_INNER)
        dt_proj_w = jax.random.normal(ks[3], (D_INNER, DT_RANK), dtype=jnp.float32) / np.sqrt(DT_RANK)
        dt_std = DT_RANK ** (-0.5)
        dt_proj_b = jax.random.uniform(ks[4], (D_INNER,), minval=-dt_std, maxval=dt_std, dtype=jnp.float32)
        return {'x': x, 'A_log': A_log, 'D': D, 'x_proj_w': x_proj_w, 'dt_proj_w': dt_proj_w, 'dt_proj_b': dt_proj_b}
    _L0_attn_in = _L0_attn_setup()

    def _L0_ffn_setup():
        import jax, jax.numpy as jnp
        import numpy as np
        TOP_K = 2
        key = jax.random.key(seed)
        ks = jax.random.split(key, 4)
        G, S, F, E, H = (4, 512, 512, 8, 512)
        return {'x': jax.random.normal(ks[0], (G, S, F), dtype=jnp.float32), 'router_logits': jax.random.normal(ks[1], (F, E), dtype=jnp.float32) * 0.02, 'gating_einsum': jax.random.normal(ks[2], (E, 2, H, F), dtype=jnp.float32) * 0.02, 'linear': jax.random.normal(ks[3], (E, H, F), dtype=jnp.float32) * 0.02, 'per_expert_scale': jnp.ones((E,), dtype=jnp.float32), 'router_scale': jnp.ones((F,), dtype=jnp.float32)}
    _L0_ffn_in = _L0_ffn_setup()
    _d = {'L0_attn_x': _L0_attn_in['x'], 'L0_attn_A_log': _L0_attn_in['A_log'], 'L0_attn_D': _L0_attn_in['D'], 'L0_attn_x_proj_w': _L0_attn_in['x_proj_w'], 'L0_attn_dt_proj_w': _L0_attn_in['dt_proj_w'], 'L0_attn_dt_proj_b': _L0_attn_in['dt_proj_b'], 'L0_ffn_router_logits': _L0_ffn_in['router_logits'], 'L0_ffn_gating_einsum': _L0_ffn_in['gating_einsum'], 'L0_ffn_linear': _L0_ffn_in['linear'], 'L0_ffn_per_expert_scale': _L0_ffn_in['per_expert_scale'], 'L0_ffn_router_scale': _L0_ffn_in['router_scale']}
    _x0 = _d['L0_attn_x']
    _d['L0_attn_x'] = jax.random.normal(jax.random.fold_in(jax.random.key(seed), 1), (1, 4096, 512), dtype=_x0.dtype)
    del _x0
    return _d

def reference(L0_attn_x, L0_attn_A_log, L0_attn_D, L0_attn_x_proj_w, L0_attn_dt_proj_w, L0_attn_dt_proj_b, L0_ffn_router_logits, L0_ffn_gating_einsum, L0_ffn_linear, L0_ffn_per_expert_scale, L0_ffn_router_scale):

    def _L0_attn_ref(x, A_log, D, x_proj_w, dt_proj_w, dt_proj_b):
        import jax, jax.numpy as jnp
        import numpy as np
        D_INNER, D_STATE, DT_RANK = (512, 16, 128)
        BATCH, SEQ = (2, 512)

        def _selective_scan(u, delta, A, B, C, D):
            dA = jnp.exp(delta[..., None] * A[None, None])
            dBu = (delta * u)[..., None] * B[:, :, None, :]

            def step(h, inp):
                dA_t, dBu_t, C_t = inp
                h = dA_t * h + dBu_t
                y_t = jnp.einsum('bdn,bn->bd', h, C_t)
                return (h, y_t)
            h0 = jnp.zeros((u.shape[0], u.shape[2], A.shape[1]), dtype=u.dtype)
            xs = (jnp.moveaxis(dA, 1, 0), jnp.moveaxis(dBu, 1, 0), jnp.moveaxis(C, 1, 0))
            _, ys = jax.lax.scan(step, h0, xs)
            y = jnp.moveaxis(ys, 0, 1)
            return y + u * D[None, None, :]
        x_dbl = jnp.einsum('bld,ed->ble', x, x_proj_w)
        delta_r = x_dbl[..., :DT_RANK]
        B = x_dbl[..., DT_RANK:DT_RANK + D_STATE]
        C = x_dbl[..., DT_RANK + D_STATE:]
        delta = jnp.einsum('blr,dr->bld', delta_r, dt_proj_w) + dt_proj_b
        delta = jax.nn.softplus(delta)
        A = -jnp.exp(A_log)
        return _selective_scan(x, delta, A, B, C, D)

    def _L0_ffn_ref(x, router_logits, gating_einsum, linear, per_expert_scale, router_scale):
        import jax, jax.numpy as jnp
        import numpy as np
        TOP_K = 2
        G, S, F = x.shape
        E = router_logits.shape[-1]
        H = linear.shape[1]
        k = TOP_K
        dtype = x.dtype
        var = jnp.mean(jnp.square(x.astype(jnp.float32)), axis=-1, keepdims=True)
        router_input = x * jax.lax.rsqrt(var + 1e-06).astype(dtype)
        root_size = jax.lax.rsqrt(jnp.array(F, dtype=dtype))
        router_input = router_input * root_size * router_scale.astype(dtype)
        logits = jnp.einsum('gsd,de->gse', router_input, router_logits.astype(dtype))
        logits32 = logits.astype(jnp.float32)
        probs = jax.nn.softmax(logits32, axis=-1)
        _, choices = jax.lax.approx_max_k(logits32, k=k)
        indicator = jax.nn.one_hot(choices, E, dtype=probs.dtype).sum(axis=-2)
        renorm = jnp.sum(indicator * probs, axis=-1, keepdims=True)
        renorm = jnp.where(renorm > 0.0, renorm, 1.0)
        weights = probs / renorm
        x_flat = x.reshape((-1, F))
        batch_size = G * S
        choices_flat = choices.ravel()
        xs_order = choices_flat.argsort()
        xs_reverse_argsort = xs_order.argsort()
        xs_indices = jnp.repeat(jnp.arange(batch_size), k)[xs_order]
        sorted_xs = x_flat[xs_indices, :]
        choices_oh = jax.nn.one_hot(choices, num_classes=E, dtype=jnp.int32)
        tokens_per_expert = jnp.sum(choices_oh, axis=(0, 1, 2))
        combine_weights = (choices_oh.astype(jnp.float32) * jnp.expand_dims(weights, axis=2)).sum(axis=-1).astype(weights.dtype)
        w_gate = jnp.transpose(gating_einsum, (0, 3, 1, 2)).reshape(E, F, 2 * H)
        gate_out = jax.lax.ragged_dot(sorted_xs, w_gate.astype(dtype), group_sizes=tokens_per_expert)
        gate_out = gate_out.reshape(gate_out.shape[0], 2, H)
        activation = jax.nn.gelu(gate_out[:, 0, :]) * gate_out[:, 1, :]
        expert_outputs = jax.lax.ragged_dot(activation, linear.astype(dtype), group_sizes=tokens_per_expert)
        expert_indices = jnp.repeat(jnp.arange(E), tokens_per_expert, total_repeat_length=expert_outputs.shape[0])
        expert_outputs = expert_outputs * per_expert_scale.astype(expert_outputs.dtype)[expert_indices, None]
        out = expert_outputs[xs_reverse_argsort].reshape((G, S, k, -1))
        out = jnp.einsum('blkd,blk->bld', out, combine_weights, preferred_element_type=out.dtype)
        return out
    x = L0_attn_x
    x = x + _L0_attn_ref(_layernorm(x, axis=-1), L0_attn_A_log, L0_attn_D, L0_attn_x_proj_w, L0_attn_dt_proj_w, L0_attn_dt_proj_b)
    x = x + _L0_ffn_ref(_layernorm(x, axis=-1), L0_ffn_router_logits, L0_ffn_gating_einsum, L0_ffn_linear, L0_ffn_per_expert_scale, L0_ffn_router_scale)
    return x

_drawn_inputs = setup_inputs


def setup_inputs(seed=0):
    import zlib

    import numpy as np

    out = dict(_drawn_inputs(seed))
    spreads = {'L0_attn_D': (1.0, 0.6),
     'L0_ffn_per_expert_scale': (1.0, 0.6),
     'L0_ffn_router_scale': (1.0, 0.6)}
    factors = {'L0_attn_dt_proj_b': 2.838,
     'L0_ffn_router_logits': 8.0,
     'L0_ffn_gating_einsum': 8.0,
     'L0_ffn_linear': 8.0}
    for name, (base, spread) in spreads.items():
        noise = np.random.default_rng([zlib.crc32(name.encode()), seed]).standard_normal(out[name].shape)
        drawn = base * np.exp(spread * noise) if base else spread * noise
        out[name] = jnp.asarray(drawn.astype(out[name].dtype))
    for name, factor in factors.items():
        out[name] = (out[name] * factor).astype(out[name].dtype)
    return out
```

```python
from contextlib import ExitStack

import concourse.bass as bass
from concourse import mybir

ALU = mybir.AluOpType
ACT = mybir.ActivationFunctionType
F32 = mybir.dt.float32
F32R = mybir.dt.float32r
I32 = mybir.dt.int32
U32 = mybir.dt.uint32
AX_X = mybir.AxisListType.X

P = 128
LN_EPS = 1e-5
RMS_EPS = 1e-6


def selective_scan_moe_kernel(nc, x, A_log, D, x_proj_T, dt_proj_T, dt_bias, router_logits,
                              expert_weights, expert_scale, router_scale, out):
    T, DM = x.shape
    NS = A_log.shape[1]
    R = dt_proj_T.shape[0]
    E = router_logits.shape[1]
    TOP_K = 2
    H = DM
    KB = DM // P
    CH = 512
    NC = T // CH
    TB = CH // P
    GB = 2
    NG = KB // GB
    UNITS = KB * NS
    UG = UNITS // NG

    REGION = T + P
    TAG = DM
    WCOL = DM + 1
    ROW = DM + 1 + E
    UN = 4
    TILES = -(-((TOP_K * T - E) // P + E) // UN) * UN
    TT = TILES + UN
    WROW = 2 * H + DM

    HR, PR, BR = 8, 4, 4
    NB = NG * NS
    BRR = 4

    ctx = ExitStack()
    with ctx:
        def sb(name, shape, dt=F32):
            return ctx.enter_context(nc.sbuf_tensor(name, shape, dt))

        def ps(name):
            return ctx.enter_context(nc.psum_tensor(name, [P, 512], F32))

        def sem(name):
            return ctx.enter_context(nc.semaphore(name))

        sorted_rows = nc.dram_tensor("sorted_rows", [E * REGION + P, ROW], F32).ap()

        ident = sb("ident", [P, P])
        before = sb("before", [P, P])
        ones = sb("ones", [P, P])
        pick = sb("pick", [64, 2 * NS, P], F32R)
        wx = sb("wx", [P, KB, R])
        wbc = sb("wbc", [P, KB, 64])
        wdt = sb("wdt", [P, DM])
        bdt = sb("bdt", [P, KB])
        a_neg = sb("a_neg", [P, KB, NS])
        d_skip = sb("d_skip", [P, KB])
        rscale = sb("rscale", [P, KB])
        wr = sb("wr", [P, KB, E])
        escale = sb("escale", [P, E])
        iota_e = sb("iota_e", [P, E])
        region_of = sb("region_of", [P, E])
        pad_rows = sb("pad_rows", [P, ROW])
        pid = sb("pid", [P, 1])

        scanned = sb("scanned", [P, 3, 2, KB, CH])
        delta, du, u = scanned[:, 0], scanned[:, 1], scanned[:, 2]
        x_in = sb("x_in", [P, 2, TB, DM])
        bc = sb("bc", [64, 2, CH], F32R)
        xn = sb("xn", [P, TB, DM])
        dr = sb("dr", [P, CH])
        zabs = sb("zabs", [P, 2, CH])
        soft = sb("soft", [P, 2, CH])
        brep = sb("brep", [P, BRR, CH])
        dbu = sb("dbu", [P, BR, CH])
        h = sb("h", [P, HR, CH])
        pick_f = h[0:64].rearrange("p r (m q) -> p (r m) q", q=P)
        prod = sb("prod", [P, PR, CH])
        state = sb("state", [P, UNITS])
        yd = sb("yd", [P, KB, CH])
        x1 = sb("x1", [P, TB, DM])
        rows = sb("rows", [P, TB, ROW])
        x2T = sb("x2T", [P, TB, KB, P])
        sq = sb("sq", [P, DM])
        st6 = sb("st6", [P, 2, TB, 6])
        mv = sb("mv", [P, 2, TB, 2])
        var_eps = sb("var_eps", [P, 2, TB])
        rstd = sb("rstd", [P, 2, TB])
        nmr = sb("nmr", [P, 2, TB])
        neg_half = sb("neg_half", [P, TB])
        msq = sb("msq", [P, TB])
        mean_sq = sb("mean_sq", [P, TB])
        rrms = sb("rrms", [P, TB])
        lg = sb("lg", [P, TB, E])
        mx = sb("mx", [P, TB, E])
        ix = sb("ix", [P, TB, E], U32)
        ixf = sb("ixf", [P, TB, TOP_K])
        ex = sb("ex", [P, TB, E])
        s1 = sb("s1", [P, TB])
        oh = sb("oh", [P, TOP_K, TB, E])
        chosen = sb("chosen", [P, TB, E])
        seen = sb("seen", [P, TB + 1, E])
        place = sb("place", [P, TB, E])
        slotf = sb("slotf", [P, TOP_K, TB])
        slot = sb("slot", [P, TOP_K, TB], I32)
        tagf = sb("tagf", [P, TB])

        cnt = sb("cnt", [P, E])
        padf = sb("padf", [P, E])
        pad_slot = sb("pad_slot", [P, E], I32)
        t_i = sb("t_i", [P, E], I32)
        nt = sb("nt", [P, E])
        incl = sb("incl", [P, E])
        excl = sb("excl", [P, E])
        zero_e = sb("zero_e", [P, E])
        jrow = sb("jrow", [1, TT])
        w3 = sb("w3", [1, TT, E])
        v3 = sb("v3", [1, TT, E])
        base_e = sb("base_e", [1, E])
        need_e = sb("need_e", [1, E])
        jt = sb("jt", [1, TT])
        t_row = sb("t_row", [1, TT], I32)
        t_exp = sb("t_exp", [1, TT], I32)
        t_load = sb("t_load", [1, TT], I32)
        t_need = sb("t_need", [1, TT], I32)
        e_f = sb("e_f", [1, TT])

        wexp = scanned[:].rearrange("p a b k c -> p (a b k c)").rearrange("p (s k w) -> p s k w", s=2, k=KB)
        xT = xn[:, 0].rearrange("p (k t) -> p k t", t=P)
        aT = xn[:, 1].rearrange("p (k t) -> p k t", t=P)
        act, g_act = xn[:, 2], xn[:, 3]
        xt = sb("xt", [P, UN, ROW])
        cw = sb("cw", [P, UN])
        tag = sb("tag", [P, UN], I32)
        ysb = x1[:, 0:2]

        bank = [ps(f"bank{i}") for i in range(8)]
        y_ps, da_ps, c_ps, b_ps, work = bank[0:2], bank[2:4], bank[4:6], bank[6], bank[7]
        xT_ps, gate_ps, up_ps, aT_ps, o_ps = bank[0], bank[1], bank[2], bank[3], bank[4]

        S = {n: sem(n) for n in (
            "waited_alone pads_placed var_ready var2_ready var_eps_ready var2_eps_ready rstd_ready rstd2_ready "
            "stats_ready stats2_ready mean_sq_ready rms_ready consts pick_ready "
            "weights_in a_exp a_ready wr_ready x_in_done xn_ready work_full work_free "
            "bc_hi z_ready exp_z_ready softplus_ready delta_ready du_ready "
            "b_full b_copied c_full da_ready dbu_ready scan_done prod_ready prod_used state_saved y_taken "
            "x1_stored x2_ready sum_sq ex_in ex_ready rows_ready slots_ready rows_out chosen_ready "
            "prologue_v epilogue_v tables_v counts tables pad_ready w_in xT_full xT_ready gu_full "
            "gelu_ready act_ready aT_full aT_ready o_full y_ready tag_ready added cw_ready").split()}
        tile_in = [sem(f"tile_in{q}") for q in range(UN)]

        block = ctx.enter_context(nc.Block())

        def alone(eng):
            eng.sem_inc(S["waited_alone"], 1)

        def wait(eng, name, count):
            if not isinstance(count, int) or count > 0:
                eng.wait_ge(S[name], count)

        class Chain:

            def __init__(self, eng, name, base=0):
                self.eng, self.name, self.base, self.k = eng, name, base, 0

            def did(self, ins):
                self.k += 1
                ins.then_inc(S[self.name], 1)

            def so_far(self):
                wait(self.eng, self.name, self.base + self.k)

            def link(self, ins):
                self.did(ins)
                self.so_far()

        LAST = NC - 1
        USES_E = [("x1", t) for t in range(TB)] + [("x2", t) for t in range(TB)] + [("logits", 0)]
        USES_U = [("u", b) for b in range(KB)]
        USES_P = [("rank_dt", 0), ("bc", 0)] + [("z", b) for b in range(KB)]

        def work_use(c, what, k=0):
            u = USES_U if c < LAST else []
            p = USES_P if c < LAST else []
            order = (USES_E + u + [("rank", 0)] if c >= 1 else u) + p
            return order.index((what, k))

        CONSTS = 3
        USES_1 = len(USES_U) + len(USES_P)
        USES_2 = len(USES_E) + 1 + USES_1
        USES_G = USES_2 - 2 * USES_1

        class Body:

            def __init__(self, c, kind):
                self.c, self.kind, self.par = c, kind, kind % 2
                if kind == -1:
                    self.uses = 0
                elif kind == 0:
                    self.uses = USES_1
                elif kind < NC:
                    self.uses = c * USES_2 - USES_G
                else:
                    self.uses = LAST * USES_2 - USES_G + len(USES_E) + 1
                self.epilogue, self.prologue = kind >= 1, kind < LAST

            def use(self, what, k=0):
                return self.uses + work_use(self.kind, what, k)

        def bodies(eng, run):
            run(Body(0, 0))
            with eng.Fori(0, (NC - 2) // 2) as pair:
                run(Body(pair * 2 + 1, 1))
                run(Body(pair * 2 + 2, 2))
            run(Body(LAST, LAST))

        def rows_sent(c):
            return 16 + c * (TB * TOP_K * 16)

        def x1_chunks(c):
            return 16 + c * 16

        PE_X1, DVE_X1, DVE_ST2, POOL_R2, DVE_N2, ACT_X2, ACT_SQ = 4, 6, 7, 18, 19, 20, 22
        PE_X2, ACT_X2T, POOL_RMS, PE_LG, DVE_LG, ACT_EX, PE_RANK, DVE_PLACE = 23, 26, 30, 32, 34, 37, 43, 44
        DVE_ST1, POOL_R1, DVE_N1, ACT_XN, PE_U, ACT_U = 17, 28, 30, 32, 35, 38
        PE_R, ACT_R, PE_BC, ACT_BC, DVE_BC, PE_Z, ACT_Z, DVE_Z = 45, 47, 47, 49, 49, 51, 54, 56
        POOL_ROWS = 49

        @block.sync
        def _(sp):
            n = 0
            for dst, src in (
                (wx[:], x_proj_T[:, 0:R].rearrange("(k p) e -> p k e", p=P)),
                (wbc[:, :, 0:32], x_proj_T[:, R:R + 2 * NS].rearrange("(k p) e -> p k e", p=P)),
                (wbc[:, :, 32:64], x_proj_T[:, R:R + 2 * NS].rearrange("(k p) e -> p k e", p=P)),
                (wdt[:], dt_proj_T),
                (bdt[:], dt_bias),
                (a_neg[:], A_log.rearrange("(k p) n -> p k n", p=P)),
                (d_skip[:], D),
                (rscale[:], router_scale),
                (wr[:], router_logits.rearrange("(k p) e -> p k e", p=P)),
                (escale[:], expert_scale.partition_broadcast(P)),
            ):
                sp.dma_start(dst, src).then_inc(S["weights_in"], 16)
                n += 1
            assert n == 10
            sp.wait_ge(S["consts"], CONSTS)
            sp.dma_start(out[T:T + P, :], pad_rows[:, 0:DM]).then_inc(S["x1_stored"], 16)

            def load_x(c, par):
                sp.dma_start(x_in[:, par], x[bass.ds(c * CH, CH), :].rearrange("(b p) d -> p b d", p=P))\
                  .then_inc(S["x_in_done"], 16)

            def store_x1(c):
                sp.dma_start(out[bass.ds(c * CH, CH), :].rearrange("(b p) d -> p b d", p=P), x1[:])\
                  .then_inc(S["x1_stored"], 16)

            def body(b):
                if b.epilogue:
                    wait(sp, "work_free", b.use("x1", TB - 1) + 1)
                    store_x1(b.c - 1)
                if b.prologue:
                    wait(sp, "x_in_done", (b.c + 1) * 16)
                    load_x(b.c + 1, 1 - b.par)

            load_x(0, 0)
            bodies(sp, body)
            wait(sp, "work_free", Body(NC, NC).use("x1", TB - 1) + 1)
            store_x1(LAST)
            wait(sp, "y_taken", NC * KB)
            sp.dma_start(wexp[:, 0], expert_weights[0]).then_inc(S["w_in"], 16)
            sp.wait_ge(S["tables"], 1)
            sp.wait_ge(S["rows_out"], rows_sent(NC))
            sp.wait_ge(S["pads_placed"], 16 * E)

            def load_tile(j, slot_):
                row = sp.value_load(t_row[0:1, bass.ds(j, 1)], min_val=0, max_val=E * REGION)
                sp.dma_start(xt[:, slot_], sorted_rows[bass.ds(row, P), :]).then_inc(tile_in[slot_], 16)

            def load_weights(j):
                sp.wait_ge(S["w_in"], j * 16 + 16)
                fresh = sp.value_load(t_load[0:1, bass.ds(j, 1)], min_val=0, max_val=E - 1)
                sp.dma_start(wexp[:, bass.ds(fresh % 2, 1)].rearrange("p a k w -> p (a k w)"),
                             expert_weights[bass.ds(fresh, 1)].rearrange("a p k w -> (a p) (k w)"),
                             cond=fresh > 0).then_inc(S["w_in"], 16)

            for q in range(UN):
                load_tile(q, q)

            def next_loads(j, q):
                wait(sp, "o_full", j)
                load_weights(j)
                sp.wait_ge(S["xT_full"], j + 1)
                sp.wait_ge(S["tag_ready"], j + 1)
                load_tile(j + UN, q)

            for q in range(UN):
                next_loads(q, q)
            with sp.Fori(1, TILES // UN) as turn:
                for q in range(UN):
                    next_loads(turn * UN + q, q)
            sp.wait_ge(S["w_in"], (TILES + 1) * 16)
            for q in range(UN):
                sp.wait_ge(tile_in[q], TT // UN * 16)

        @block.gpsimd
        def _(gp):
            own = Chain(gp, "consts")
            gp.memset(ident[:], 0.0)
            gp.memset(before[:], 1.0)
            gp.memset(pick_f, 0.0)
            gp.memset(pad_rows[:], 0.0)
            gp.memset(zero_e[:], 0.0)
            gp.memset(neg_half[:], -0.5)
            gp.memset(state[:], 0.0)
            gp.memset(seen[:, TB, :], 0.0)
            own.link(gp.memset(ones[:], 1.0))
            gp.affine_select(out=ident[:], in_=ident[:], compare_op=ALU.not_equal, fill=1.0, base=0,
                             pattern=[[-1, P]], channel_multiplier=1)
            gp.affine_select(out=before[:], in_=before[:], compare_op=ALU.is_gt, fill=0.0, base=0,
                             pattern=[[1, P]], channel_multiplier=-1)
            own.link(gp.affine_select(out=pick_f, in_=pick_f, compare_op=ALU.not_equal, fill=1.0, base=0,
                                      pattern=[[-1, 2 * NS], [0, P]], channel_multiplier=1))
            gp.affine_select(out=pick_f, in_=pick_f, compare_op=ALU.not_equal, fill=1.0, base=-32,
                             pattern=[[-1, 2 * NS], [0, P]], channel_multiplier=1)
            gp.iota(iota_e[:], pattern=[[1, E]], base=0, channel_multiplier=0, allow_small_or_imprecise_dtypes=True)
            gp.iota(region_of[:], pattern=[[REGION, E]], base=0, channel_multiplier=0, allow_small_or_imprecise_dtypes=True)
            gp.iota(pid[:], pattern=[[0, 1]], base=0, channel_multiplier=1, allow_small_or_imprecise_dtypes=True)
            gp.iota(tagf[:], pattern=[[P, TB]], base=0, channel_multiplier=1, allow_small_or_imprecise_dtypes=True)
            gp.iota(jrow[:], pattern=[[1, TT]], base=0, channel_multiplier=0, allow_small_or_imprecise_dtypes=True)
            gp.iota(pad_rows[:, TAG:TAG + 1].bitcast(I32), pattern=[[0, 1]], base=T, channel_multiplier=1)\
              .then_inc(S["consts"], 1)

            gp.wait_ge(S["consts"], CONSTS)
            gp.dma_start(sorted_rows[E * REGION:E * REGION + P, :], pad_rows[:]).then_inc(S["rows_out"], 16)

            def inverse_root(which, signal, done, ready, count):
                wait(gp, signal, count)
                alone(gp)
                gp.tensor_scalar(var_eps[:, which], mv[:, which, :, 1], LN_EPS, None, ALU.add).then_inc(S[done], 1)
                wait(gp, done, count)
                gp.tensor_tensor(rstd[:, which], var_eps[:, which], neg_half[:], ALU.pow).then_inc(S[ready], 1)

            def inverse_rms(c):
                wait(gp, "sum_sq", c * TB + TB)
                alone(gp)
                gp.tensor_scalar(mean_sq[:], msq[:], 1.0 / DM, RMS_EPS, ALU.mult, ALU.add).then_inc(S["mean_sq_ready"], 1)
                wait(gp, "mean_sq_ready", c + 1)
                gp.tensor_tensor(rrms[:], mean_sq[:], neg_half[:], ALU.pow).then_inc(S["rms_ready"], 1)

            def send_rows(c, k):
                if k == 0:
                    wait(gp, "slots_ready", c + 1)
                    wait(gp, "rows_ready", c + 1)
                    alone(gp)
                gp.indirect_dma_start(out=sorted_rows,
                                      out_offset=bass.IndirectOffsetOnAxis(ap=slot[:, k % TOP_K, k // TOP_K:k // TOP_K + 1], axis=0),
                                      in_=rows[:, k // TOP_K, :], in_offset=None).then_inc(S["rows_out"], 16)

            def body(b):
                c = b.c
                for i in range(UNITS):
                    g, n, dd = i // UG, i % UG // GB, i % GB
                    q = g * GB + dd
                    if dd == 0:
                        wait(gp, "b_copied", c * NB + (g * NS + n + 1))
                    if n == 0:
                        wait(gp, "du_ready", c * KB + (q + 1))
                    wait(gp, "scan_done", c * UNITS + (i - BR + 1))
                    gp.tensor_tensor(dbu[:, i % BR],
                                     du[:, b.par, q], brep[:, (g * NS + n) % BRR], ALU.mult).then_inc(S["dbu_ready"], 1)
                    if b.epilogue and i == POOL_R2:
                        inverse_root(1, "var2_ready", "var2_eps_ready", "rstd2_ready", c)
                    if b.prologue and i == POOL_R1:
                        inverse_root(0, "var_ready", "var_eps_ready", "rstd_ready", c + 2)
                    if b.epilogue and i == POOL_RMS:
                        inverse_rms(c - 1)
                    if b.epilogue and i in range(POOL_ROWS, POOL_ROWS + 2 * TB * TOP_K, 2):
                        send_rows(c - 1, (i - POOL_ROWS) // 2)

            inverse_root(0, "var_ready", "var_eps_ready", "rstd_ready", 1)
            bodies(gp, body)
            inverse_root(1, "var2_ready", "var2_eps_ready", "rstd2_ready", NC)
            inverse_rms(LAST)
            for k in range(TB * TOP_K):
                send_rows(LAST, k)
            gp.wait_ge(S["pad_ready"], 1)
            for e in range(E):
                gp.indirect_dma_start(out=sorted_rows, out_offset=bass.IndirectOffsetOnAxis(ap=pad_slot[:, e:e + 1], axis=0),
                                      in_=pad_rows[:], in_offset=None).then_inc(S["pads_placed"], 16)
            gp.wait_ge(S["x1_stored"], x1_chunks(NC))

            def add_tile(j, q):
                gp.wait_ge(S["tag_ready"], j + 1)
                gp.wait_ge(S["y_ready"], j + 1)
                wait(gp, "added", j * 16)
                alone(gp)
                gp.indirect_dma_start(out=out, out_offset=bass.IndirectOffsetOnAxis(ap=tag[:, q:q + 1], axis=0),
                                      in_=ysb[:, q % 2], in_offset=None, compute_op=ALU.add).then_inc(S["added"], 16)

            for q in range(UN):
                add_tile(q, q)
            with gp.Fori(1, TILES // UN) as turn:
                for q in range(UN):
                    add_tile(turn * UN + q, q)
            gp.wait_ge(S["added"], 16 * TILES)

        @block.scalar
        def _(ac):
            nc.scalar.preload_act_table_set("natural_log_exp_and_others")
            ac.wait_ge(S["weights_in"], 160)
            nc.scalar.activation(a_neg[:], a_neg[:], ACT.Exp).then_inc(S["a_exp"], 1)
            ac.wait_ge(S["a_ready"], 1)

            def norm_x(c, par, t, transposed):
                if t == 0:
                    wait(ac, "stats_ready", c + 1)
                    wait(ac, "work_full", transposed)
                nc.scalar.activation(xn[:, t], x_in[:, par, t], ACT.Identity, bias=nmr[:, 0, t:t + 1],
                                     scale=rstd[:, 0, t:t + 1]).then_inc(S["xn_ready"], 1)

            def take(b, what, k=0):
                wait(ac, "work_full", b.use(what, k) + 1)

            def copy_u(b, c, par, k):
                take(b, "u", k)
                if k == 0:
                    wait(ac, "y_taken", (c - 1) * KB)
                nc.scalar.copy(u[:, par, k], work[:]).then_inc(S["work_free"], 1)

            def copy_r(b):
                take(b, "rank_dt")
                nc.scalar.copy(dr[:], work[:]).then_inc(S["work_free"], 1)

            def copy_bc(b, par):
                take(b, "bc")
                nc.scalar.copy(bc[:, par], work[0:64, :]).then_inc(S["bc_hi"], 1)

            def softplus_1(b, c, par, k):
                take(b, "z", k)
                wait(ac, "exp_z_ready", c * KB + (k - 1))
                wait(ac, "softplus_ready", c * KB + (k - 1))
                if k == 0:
                    wait(ac, "da_ready", (c - 1) * UNITS)
                nc.scalar.activation(zabs[:, k % 2], work[:], ACT.Abs, bias=bdt[:, k:k + 1]).then_inc(S["z_ready"], 1)
                nc.scalar.activation(delta[:, par, k], work[:], ACT.Relu, bias=bdt[:, k:k + 1]).then_inc(S["work_free"], 1)
                wait(ac, "z_ready", c * KB + (k + 1))
                nc.scalar.activation(zabs[:, k % 2], zabs[:, k % 2], ACT.Exp, scale=-1.0).then_inc(S["exp_z_ready"], 1)

            def softplus_2(c, k):
                wait(ac, "exp_z_ready", c * KB + (k + 1))
                wait(ac, "delta_ready", c * KB + (k - 1))
                nc.scalar.activation(soft[:, k % 2], zabs[:, k % 2], ACT.Ln, bias=1.0).then_inc(S["softplus_ready"], 1)

            def copy_b(c, m):
                count = c * NB + m
                wait(ac, "b_full", count + 1)
                wait(ac, "dbu_ready", (count - (BRR - 1)) * GB)
                nc.scalar.copy(brep[:, m % BRR], b_ps[:]).then_inc(S["b_copied"], 1)

            def save_states(c, q):
                wait(ac, "scan_done", c * UNITS + (4 * q + 4))
                nc.scalar.copy(state[:, 4 * q:4 * q + 4], h[:, 4 * q % HR:4 * q % HR + 4, CH - 1]).then_inc(S["state_saved"], 1)

            def norm_x1(c, t):
                if t == 0:
                    wait(ac, "stats2_ready", c + 1)
                    wait(ac, "rows_out", rows_sent(c))
                nc.scalar.activation(rows[:, t, 0:DM], x1[:, t], ACT.Identity, bias=nmr[:, 1, t:t + 1],
                                     scale=rstd[:, 1, t:t + 1]).then_inc(S["x2_ready"], 1)

            def square(c, t):
                wait(ac, "x2_ready", c * TB + (t + 1))
                if t > 0:
                    wait(ac, "sum_sq", c * TB + t)
                nc.scalar.activation(sq[:], rows[:, t, 0:DM], ACT.Square, accum_out=msq[:, t:t + 1]).then_inc(S["sum_sq"], 1)

            def copy_x2T(b, t):
                take(b, "x2", t)
                nc.scalar.copy(x2T[:, t].rearrange("p k t -> p (k t)"), work[:]).then_inc(S["work_free"], 1)

            def exps(c):
                wait(ac, "ex_in", c + 1)
                nc.scalar.activation(ex[:], ex[:], ACT.Exp).then_inc(S["ex_ready"], 1)

            def body(b):
                c = b.c
                for i in range(UNITS):
                    g, n, dd = i // UG, i % UG // GB, i % GB
                    q = g * GB + dd
                    m = g * NS + n
                    if dd == 0 and (b.prologue or m + 2 < NB):
                        copy_b(c, m + 2)
                    if n == 0:
                        wait(ac, "delta_ready", c * KB + (q + 1))
                    wait(ac, "scan_done", c * UNITS + (i - 1))
                    nc.scalar.activation(da_ps[i % 2][:], delta[:, b.par, q], ACT.Exp,
                                         scale=a_neg[:, q, n:n + 1]).then_inc(S["da_ready"], 1)
                    if i >= 6 and i % 4 == 2:
                        save_states(c, (i - 6) // 4)
                    if i == 2 and b.kind >= 1:
                        save_states(c - 1, UNITS // 4 - 1)
                    if b.epilogue:
                        if i in range(ACT_X2, ACT_X2 + TB):
                            norm_x1(c - 1, i - ACT_X2)
                        if i in range(ACT_SQ, ACT_SQ + TB):
                            square(c - 1, i - ACT_SQ)
                        if i in range(ACT_X2T, ACT_X2T + 2 * TB, 2):
                            copy_x2T(b, (i - ACT_X2T) // 2)
                        if i == ACT_EX:
                            exps(c - 1)
                    if b.prologue:
                        if i in range(ACT_XN, ACT_XN + TB):
                            norm_x(c + 1, 1 - b.par, i - ACT_XN, b.uses)
                        if i in range(ACT_U, ACT_U + 2 * KB, 2):
                            copy_u(b, c + 1, 1 - b.par, (i - ACT_U) // 2)
                        if i == ACT_R:
                            copy_r(b)
                        if i == ACT_BC:
                            copy_bc(b, 1 - b.par)
                        if i in range(ACT_Z, ACT_Z + 2 * KB, 2):
                            softplus_1(b, c + 1, 1 - b.par, (i - ACT_Z) // 2)
                        if i in range(ACT_Z + 1, ACT_Z + 1 + 2 * KB, 2):
                            softplus_2(c + 1, (i - ACT_Z - 1) // 2)

            first = Body(-1, -1)
            for t in range(TB):
                norm_x(0, 0, t, 0)
            for k in range(KB):
                copy_u(first, 0, 0, k)
            copy_r(first)
            copy_bc(first, 0)
            for k in range(KB):
                softplus_1(first, 0, 0, k)
                softplus_2(0, k)
            for m in range(2):
                copy_b(0, m)
            bodies(ac, body)
            last = Body(NC, NC)
            for t in range(TB):
                norm_x1(LAST, t)
            for t in range(TB):
                square(LAST, t)
            for t in range(TB):
                copy_x2T(last, t)
            exps(LAST)

            def copy_xT(j):
                ac.wait_ge(S["xT_full"], j + 1)
                nc.scalar.copy(xT.rearrange("p k t -> p (k t)"), xT_ps[:]).then_inc(S["xT_ready"], 1)

            def gelu(j):
                ac.wait_ge(S["gu_full"], j + 1)
                nc.scalar.activation(g_act, gate_ps[:], ACT.Gelu_apprx_tanh).then_inc(S["gelu_ready"], 1)

            def copy_aT(j):
                ac.wait_ge(S["aT_full"], j + 1)
                nc.scalar.copy(aT.rearrange("p k t -> p (k t)"), aT_ps[:]).then_inc(S["aT_ready"], 1)

            def tile(j, prev):
                copy_aT(prev)
                gelu(j)

            copy_xT(0)
            gelu(0)
            copy_xT(1)
            with ac.Fori(0, (TILES - UN) // UN) as turn:
                for q in range(UN):
                    tile(turn * UN + (q + 1), turn * UN + q)
                    copy_xT(turn * UN + (q + 2))
            for j in range(TILES - UN + 1, TILES):
                tile(j, j - 1)
                if j + 1 < TILES:
                    copy_xT(j + 1)
            copy_aT(TILES - 1)

        @block.vector
        def _(dv):
            dv.wait_ge(S["consts"], CONSTS)
            nc.vector.tensor_copy(pick[:], pick_f).then_inc(S["pick_ready"], 1)
            dv.wait_ge(S["a_exp"], 1)
            nc.vector.tensor_scalar(a_neg[:], a_neg[:], -1.0, None, ALU.mult).then_inc(S["a_ready"], 1)
            for k in range(KB):
                nc.vector.tensor_scalar(wr[:, k], wr[:, k], rscale[:, k:k + 1], float(DM) ** -0.5, ALU.mult,
                                        ALU.mult).then_inc(S["wr_ready"], 1)

            def take(b, what, k=0):
                wait(dv, "work_full", b.use(what, k) + 1)

            def stats(own, which, src, t):
                own.did(nc.vector.bn_stats(st6[:, which, t], src))

            def aggregate(own, which, t, signal):
                own.so_far()
                alone(dv)
                last = nc.vector.bn_aggr(mv[:, which, t], st6[:, which, t])
                if t == TB - 1:
                    last.then_inc(S[signal], 1)
                else:
                    own.did(last)

            def shift(which, signal, done, count):
                wait(dv, signal, count)
                nc.vector.scalar_tensor_tensor(nmr[:, which], mv[:, which, :, 0], -1.0, rstd[:, which], ALU.mult, ALU.mult)\
                  .then_inc(S[done], 1)

            def split_bc(c, par):
                wait(dv, "bc_hi", c + 1)
                nc.vector.tensor_tensor(bc[32:64, par], work[32:64, :], bc[32:64, par].bitcast(F32), ALU.subtract)\
                  .then_inc(S["work_free"], 1)

            def time_step(c, par, k):
                wait(dv, "softplus_ready", c * KB + (k + 1))
                nc.vector.tensor_tensor(delta[:, par, k], delta[:, par, k], soft[:, k % 2], ALU.add).then_inc(S["delta_ready"], 1)
                wait(dv, "delta_ready", c * KB + (k + 1))
                nc.vector.tensor_tensor(du[:, par, k], delta[:, par, k], u[:, par, k], ALU.mult).then_inc(S["du_ready"], 1)

            def scan(b, i):
                c = b.c
                wait(dv, "da_ready", c * UNITS + (i + 1))
                wait(dv, "dbu_ready", c * UNITS + (i + 1))
                if i % 4 == 0:
                    wait(dv, "state_saved", c * (UNITS // 4) + (i // 4 - 1))
                if i < HR:
                    wait(dv, "prod_ready", c * UNITS + (i - HR + 1))
                nc.vector.tensor_tensor_scan(h[:, i % HR], da_ps[i % 2][:],
                                             dbu[:, i % BR],
                                             state[:, i:i + 1], ALU.mult, ALU.add).then_inc(S["scan_done"], 1)

            def times_c(b, i):
                c, g, n, dd = b.c, i // UG, i % UG // GB, i % GB
                if dd == 0:
                    wait(dv, "c_full", c * NB + (g * NS + n + 1))
                wait(dv, "scan_done", c * UNITS + (i + 1))
                wait(dv, "prod_used", c * UNITS + (i - PR + 1))
                nc.vector.tensor_tensor(prod[:, i % PR], h[:, i % HR], c_ps[n % 2][:], ALU.mult).then_inc(S["prod_ready"], 1)

            def take_y(c, par, q):
                g, dd = q // GB, q % GB
                wait(dv, "prod_used", c * UNITS + ((g + 1) * UG - (GB - 1 - dd)))
                nc.vector.scalar_tensor_tensor(yd[:, q], u[:, par, q], d_skip[:, q:q + 1], y_ps[dd][:],
                                               ALU.mult, ALU.add).then_inc(S["y_taken"], 1)

            def residual(b, c, par, t):
                take(b, "x1", t)
                if t == 0:
                    wait(dv, "x1_stored", x1_chunks(c))
                nc.vector.tensor_tensor(x1[:, t], work[:], x_in[:, par, t], ALU.add).then_inc(S["work_free"], 1)

            def per_token(v):
                return v.unsqueeze(2).broadcast_to([P, TB, E])

            def route(b, c, own, k):
                V = nc.vector
                if k == 0:
                    wait(dv, "rms_ready", c + 1)
                    take(b, "logits")
                    V.tensor_tensor(lg[:], work[:, 0:TB * E].rearrange("p (b e) -> p b e", e=E), per_token(rrms[:]),
                                    ALU.mult).then_inc(S["work_free"], 1)
                    return
                if k == 1:
                    wait(dv, "work_free", b.use("logits") + 1)
                else:
                    own.so_far()
                if k == 1:
                    alone(dv)
                    for t in range(TB):
                        own.did(V.max(mx[:, t], lg[:, t]))
                elif k == 2:
                    alone(dv)
                    for t in range(TB):
                        own.did(V.max_index(ix[:, t], mx[:, t], lg[:, t]))
                elif k == 3:
                    V.tensor_tensor(ex[:], lg[:], mx[:, :, 0:1].broadcast_to([P, TB, E]), ALU.subtract).then_inc(S["ex_in"], 1)
                    own.did(V.tensor_copy(ixf[:], ix[:, :, 0:TOP_K]))
                elif k == 4:
                    for j in range(TOP_K):
                        own.did(V.tensor_tensor(oh[:, j], iota_e[:].unsqueeze(1).broadcast_to([P, TB, E]),
                                                ixf[:, :, j:j + 1].broadcast_to([P, TB, E]), ALU.is_equal))
                elif k == 5:
                    own.did(V.tensor_tensor(chosen[:], oh[:, 0], oh[:, 1], ALU.add))
                elif k == 6:
                    own.did(V.tensor_copy(seen[:, 0], seen[:, TB]))
                elif k <= 10:
                    t = k - 7
                    last = V.tensor_tensor(seen[:, t + 1], seen[:, t], chosen[:, t], ALU.add)
                    if t == TB - 1:
                        last.then_inc(S["chosen_ready"], 1)
                    else:
                        own.did(last)
                elif k == 11:
                    wait(dv, "ex_ready", c + 1)
                    own.did(V.tensor_reduce(s1[:], ex[:], axis=AX_X, op=ALU.add))
                elif k in (12, 16):
                    own.did(V.reciprocal(s1[:], s1[:]))
                elif k in (13, 17):
                    own.did(V.tensor_tensor(ex[:], ex[:], per_token(s1[:]), ALU.mult))
                elif k == 14:
                    own.did(V.tensor_tensor(ex[:], ex[:], chosen[:], ALU.mult))
                elif k == 15:
                    own.did(V.tensor_reduce(s1[:], ex[:], axis=AX_X, op=ALU.add))
                elif k == 18:
                    wait(dv, "rows_out", rows_sent(c))
                    own.did(V.tensor_tensor(rows[:, :, WCOL:WCOL + E], ex[:],
                                            escale[:].unsqueeze(1).broadcast_to([P, TB, E]), ALU.mult))
                elif k == 19:
                    own.did(V.tensor_copy(rows[:, :, TAG:TAG + 1].bitcast(I32), tagf[:].unsqueeze(2)))
                elif k == 20:
                    V.tensor_scalar(tagf[:], tagf[:], float(CH), None, ALU.add).then_inc(S["rows_ready"], 1)

            def places(b, c, own, k):
                V = nc.vector
                if k == 0:
                    take(b, "rank")
                    V.tensor_tensor(place[:], work[:, 0:TB * E].rearrange("p (b e) -> p b e", e=E),
                                    region_of[:].unsqueeze(1).broadcast_to([P, TB, E]), ALU.add).then_inc(S["work_free"], 1)
                    return
                if k == 1:
                    wait(dv, "work_free", b.use("rank") + 1)
                own.so_far()
                if k == 1:
                    for j in range(TOP_K):
                        own.did(V.tensor_tensor(oh[:, j], oh[:, j], place[:], ALU.mult))
                elif k == 2:
                    for j in range(TOP_K):
                        own.did(V.tensor_reduce(slotf[:, j], oh[:, j], axis=AX_X, op=ALU.add))
                elif k == 3:
                    V.tensor_copy(slot[:], slotf[:]).then_inc(S["slots_ready"], 1)

            STEPS = 21
            PER_P = 2 * TB - 1
            PER_E = 2 * TB - 1 + 29

            def body(b):
                c = b.c
                own_e = Chain(dv, "epilogue_v", (c - 1) * PER_E) if b.epilogue else None
                own_p = Chain(dv, "prologue_v", (c + 1) * PER_P) if b.prologue else None
                scan(b, 0)
                for i in range(UNITS):
                    g, n, dd = i // UG, i % UG // GB, i % GB
                    if i + 1 < UNITS:
                        scan(b, i + 1)
                    times_c(b, i)
                    if n == NS - 1 and dd == GB - 1:
                        take_y(c, b.par, g * GB)
                    if n == 0 and dd == 0 and g > 0:
                        take_y(c, b.par, g * GB - 1)
                    if i == 0 and b.kind >= 1:
                        take_y(c - 1, 1 - b.par, KB - 1)
                    if b.epilogue:
                        if i in range(DVE_X1, DVE_X1 + 2 * TB, 2):
                            residual(b, c - 1, 1 - b.par, (i - DVE_X1) // 2)
                        if i in range(DVE_ST2, DVE_ST2 + 2 * TB, 2):
                            t = (i - DVE_ST2) // 2
                            wait(dv, "work_free", b.use("x1", t) + 1)
                            stats(own_e, 1, x1[:, t], t)
                        if i in range(DVE_ST2 + 1, DVE_ST2 + 1 + 2 * TB, 2):
                            aggregate(own_e, 1, (i - DVE_ST2 - 1) // 2, "var2_ready")
                        if i == DVE_N2:
                            shift(1, "rstd2_ready", "stats2_ready", c)
                        for k in range(2 * (i - DVE_LG), 2 * (i - DVE_LG) + 2):
                            if k in range(STEPS):
                                route(b, c - 1, own_e, k)
                        if i in range(DVE_PLACE, DVE_PLACE + 4):
                            places(b, c - 1, own_e, i - DVE_PLACE)
                    if b.prologue:
                        if i in range(DVE_ST1, DVE_ST1 + TB):
                            if i == DVE_ST1:
                                wait(dv, "x_in_done", (c + 2) * 16)
                                wait(dv, "stats_ready", c + 1)
                            stats(own_p, 0, x_in[:, 1 - b.par, i - DVE_ST1], i - DVE_ST1)
                        if i in range(DVE_ST1 + TB, DVE_ST1 + 2 * TB):
                            aggregate(own_p, 0, i - DVE_ST1 - TB, "var_ready")
                        if i == DVE_N1:
                            shift(0, "rstd_ready", "stats_ready", c + 2)
                        if i == DVE_BC:
                            split_bc(c + 1, 1 - b.par)
                        if i in range(DVE_Z, DVE_Z + 2 * KB, 2):
                            time_step(c + 1, 1 - b.par, (i - DVE_Z) // 2)
                assert own_p is None or own_p.k == PER_P, own_p.k
                assert own_e is None or own_e.k == PER_E, own_e.k

            own = Chain(dv, "prologue_v", 0)
            dv.wait_ge(S["x_in_done"], 16)
            for t in range(TB):
                stats(own, 0, x_in[:, 0, t], t)
            for t in range(TB):
                aggregate(own, 0, t, "var_ready")
            shift(0, "rstd_ready", "stats_ready", 1)
            split_bc(0, 0)
            for k in range(KB):
                time_step(0, 0, k)
            bodies(dv, body)
            last = Body(NC, NC)
            own = Chain(dv, "epilogue_v", LAST * PER_E)
            take_y(LAST, LAST % 2, KB - 1)
            for t in range(TB):
                residual(last, LAST, LAST % 2, t)
                wait(dv, "work_free", last.use("x1", t) + 1)
                stats(own, 1, x1[:, t], t)
            for t in range(TB):
                aggregate(own, 1, t, "var2_ready")
            shift(1, "rstd2_ready", "stats2_ready", NC)
            for k in range(STEPS):
                route(last, LAST, own, k)
            for k in range(4):
                places(last, LAST, own, k)
            assert own.k == PER_E, own.k

            own = Chain(dv, "tables_v")
            dv.wait_ge(S["counts"], 1)
            own.link(nc.vector.tensor_copy(cnt[:], work[:, 0:E]))
            own.link(nc.vector.tensor_tensor(padf[:], cnt[:], region_of[:], ALU.add))
            own.link(nc.vector.tensor_scalar(padf[:], padf[:], pid[:], None, ALU.add))
            nc.vector.tensor_copy(pad_slot[:], padf[:]).then_inc(S["pad_ready"], 1)
            own.link(nc.vector.tensor_scalar(nt[:], cnt[:], float(P - 1), None, ALU.add))
            own.link(nc.vector.tensor_copy(t_i[:], nt[:]))
            own.link(nc.vector.tensor_scalar(t_i[:], t_i[:], P.bit_length() - 1, None, ALU.arith_shift_right))
            own.link(nc.vector.tensor_copy(nt[:], t_i[:]))
            own.link(nc.vector.tensor_scalar(nt[:], nt[:], 1.0, None, ALU.max))
            own.link(nc.vector.tensor_tensor_scan(incl[:], nt[:], zero_e[:], 0.0, ALU.add, ALU.add))
            own.link(nc.vector.tensor_tensor(excl[:], incl[:], nt[:], ALU.subtract))
            own.link(nc.vector.scalar_tensor_tensor(base_e[:], excl[0:1, :], float(-P), region_of[0:1, :], ALU.mult, ALU.add))
            own.link(nc.vector.memset(need_e[:], 16.0))
            own.link(nc.vector.tensor_scalar(need_e[:, 1:E], excl[0:1, 0:E - 1], 2.0, 16.0, ALU.add, ALU.mult))
            J = jrow[:].unsqueeze(2).broadcast_to([1, TT, E])

            def per_tile(v):
                return v.unsqueeze(1).broadcast_to([1, TT, E])

            own.link(nc.vector.tensor_tensor(w3[:], J, per_tile(incl[0:1, :]), ALU.is_ge))
            own.link(nc.vector.tensor_reduce(e_f[:], w3[:], axis=AX_X, op=ALU.add))
            own.link(nc.vector.tensor_scalar(jt[:], e_f[:], float(E - 1), None, ALU.min))
            own.link(nc.vector.tensor_copy(t_exp[:], jt[:]))
            own.link(nc.vector.tensor_tensor(w3[:], iota_e[0:1, :].unsqueeze(1).broadcast_to([1, TT, E]),
                                             e_f[:].unsqueeze(2).broadcast_to([1, TT, E]), ALU.is_equal))
            own.link(nc.vector.tensor_tensor(v3[:], w3[:], per_tile(need_e[:]), ALU.mult))
            own.link(nc.vector.tensor_reduce(jt[:], v3[:], axis=AX_X, op=ALU.add))
            own.link(nc.vector.tensor_scalar(jt[:], jt[:], 16.0, None, ALU.max))
            own.link(nc.vector.tensor_copy(t_need[:], jt[:]))
            own.link(nc.vector.tensor_scalar(v3[:], J, float(P), None, ALU.mult))
            own.link(nc.vector.tensor_tensor(v3[:], v3[:], per_tile(base_e[:]), ALU.add))
            own.link(nc.vector.tensor_tensor(v3[:], v3[:], w3[:], ALU.mult))
            own.link(nc.vector.tensor_reduce(jt[:], v3[:], axis=AX_X, op=ALU.add))
            own.link(nc.vector.tensor_scalar(e_f[:], e_f[:], float(E), float(E * REGION), ALU.is_equal, ALU.mult))
            own.link(nc.vector.tensor_tensor(jt[:], jt[:], e_f[:], ALU.add))
            own.link(nc.vector.tensor_copy(t_row[:], jt[:]))
            own.link(nc.vector.tensor_tensor(w3[:], J, per_tile(excl[0:1, :]), ALU.is_equal))
            own.link(nc.vector.tensor_scalar(v3[:], iota_e[0:1, :].unsqueeze(1).broadcast_to([1, TT, E]), 1.0, None, ALU.add))
            own.link(nc.vector.tensor_tensor(w3[:], w3[:], v3[:], ALU.mult))
            own.link(nc.vector.tensor_reduce(jt[:], w3[:], axis=AX_X, op=ALU.add))
            own.link(nc.vector.tensor_scalar(e_f[:], jt[:], float(E), None, ALU.is_lt))
            own.link(nc.vector.tensor_tensor(jt[:], jt[:], e_f[:], ALU.mult))
            nc.vector.tensor_copy(t_load[:], jt[:]).then_inc(S["tables"], 1)

            def tags(j, q, loads):
                e_j = dv.value_load(t_exp[0:1, bass.ds(j, 1)], min_val=0, max_val=E - 1)
                dv.wait_ge(tile_in[q], loads * 16)
                nc.vector.tensor_copy(cw[:, q:q + 1], xt[:, q, bass.ds(e_j + WCOL, 1)]).then_inc(S["cw_ready"], 1)
                nc.vector.tensor_copy(tag[:, q:q + 1], xt[:, q, TAG:TAG + 1].bitcast(I32)).then_inc(S["tag_ready"], 1)

            def gate(j):
                dv.wait_ge(S["gelu_ready"], j + 1)
                nc.vector.tensor_tensor(act, g_act, up_ps[:], ALU.mult).then_inc(S["act_ready"], 1)

            def weigh(j, q):
                dv.wait_ge(S["o_full"], j + 1)
                dv.wait_ge(S["cw_ready"], j + 1)
                if isinstance(j, int) and j < 2:
                    pass
                else:
                    dv.wait_ge(S["added"], j * 16 - 16)
                nc.vector.tensor_scalar(ysb[:, q % 2], o_ps[:], cw[:, q:q + 1], None, ALU.mult).then_inc(S["y_ready"], 1)

            tags(0, 0, 1)
            gate(0)
            tags(1, 1, 1)
            gate(1)
            weigh(0, 0)
            with dv.Fori(0, (TILES - UN) // UN) as turn:
                for q in range(UN):
                    j = turn * UN + (q + 2)
                    tags(j, (q + 2) % UN, turn + ((q + 2) // UN + 1))
                    gate(j)
                    weigh(turn * UN + (q + 1), (q + 1) % UN)
            for j in range(TILES - UN + 2, TILES):
                tags(j, j % UN, j // UN + 1)
                gate(j)
                weigh(j - 1, (j - 1) % UN)
            weigh(TILES - 1, (TILES - 1) % UN)

        @block.tensor
        def _(pe):
            pe.wait_ge(S["consts"], CONSTS)
            pe.wait_ge(S["pick_ready"], 1)
            pe.wait_ge(S["weights_in"], 160)
            pe.wait_ge(S["wr_ready"], KB)

            def use(b, what, k=0):
                wait(pe, "work_free", b.use(what, k))

            def transpose_xn(b, c, k):
                if k == 0:
                    wait(pe, "xn_ready", c * TB + TB)
                use(b, "u", k)
                for t in range(TB):
                    last = nc.tensor.transpose(work[:, t * P:(t + 1) * P], xn[:, t, k * P:(k + 1) * P], ident[:])
                last.then_inc(S["work_full"], 1)

            def project(b, par, what, w, rows_):
                use(b, what)
                for k in range(KB):
                    last = nc.tensor.matmul(work[0:rows_, :], w[:, k, :], u[:, par, k, :], start=k == 0, stop=k == KB - 1)
                last.then_inc(S["work_full"], 1)

            def time_rank(b, k):
                use(b, "z", k)
                nc.tensor.matmul(work[:], wdt[:, k * P:(k + 1) * P], dr[:], start=True, stop=True)\
                  .then_inc(S["work_full"], 1)

            def spread_b(c, m, par):
                wait(pe, "b_copied", c * NB + m)
                nc.tensor.matmul(b_ps[:], pick[:, m % NS], bc[:, par], start=True, stop=True).then_inc(S["b_full"], 1)

            def spread_c(c, m, par):
                wait(pe, "prod_ready", (c * NB + (m - 1)) * GB)
                nc.tensor.matmul(c_ps[m % 2][:], pick[:, NS + m % NS], bc[:, par], start=True, stop=True)\
                  .then_inc(S["c_full"], 1)

            def transpose_yd(b, c, t):
                if t == 0:
                    wait(pe, "y_taken", c * KB + KB)
                use(b, "x1", t)
                for k in range(KB):
                    last = nc.tensor.transpose(work[:, k * P:(k + 1) * P], yd[:, k, t * P:(t + 1) * P], ident[:])
                last.then_inc(S["work_full"], 1)

            def transpose_x2(b, c, t):
                wait(pe, "x2_ready", c * TB + (t + 1))
                use(b, "x2", t)
                for k in range(KB):
                    last = nc.tensor.transpose(work[:, k * P:(k + 1) * P], rows[:, t, k * P:(k + 1) * P], ident[:])
                last.then_inc(S["work_full"], 1)

            def logits(b):
                use(b, "logits")
                for t in range(TB):
                    for k in range(KB):
                        last = nc.tensor.matmul(work[:, t * E:(t + 1) * E], x2T[:, t, k, :], wr[:, k, :],
                                                start=k == 0, stop=k == KB - 1)
                last.then_inc(S["work_full"], 1)

            def rank(b, c):
                use(b, "rank")
                wait(pe, "chosen_ready", c + 1)
                nc.tensor.matmul(work[:, 0:TB * E], before[:], chosen[:].rearrange("p b e -> p (b e)"), start=True, stop=False)
                nc.tensor.matmul(work[:, 0:TB * E], ones[:], seen[:, 0:TB].rearrange("p b e -> p (b e)"), start=False,
                                 stop=True).then_inc(S["work_full"], 1)

            def body(b):
                c = b.c
                for i in range(UNITS):
                    g, n, dd = i // UG, i % UG // GB, i % GB
                    m = g * NS + n
                    if dd == GB - 1:
                        for ahead, spread in ((4, spread_b), (2, spread_c)):
                            if m + ahead < NB or b.prologue:
                                spread(c, m + ahead, b.par if m + ahead < NB else 1 - b.par)
                    if n == 0:
                        wait(pe, "y_taken", c * KB + (g * GB + dd - 1))
                    wait(pe, "prod_ready", c * UNITS + (i + 1))
                    nc.tensor.matmul(y_ps[dd][:], ident[:], prod[:, i % PR], start=n == 0, stop=n == NS - 1)\
                      .then_inc(S["prod_used"], 1)
                    if b.epilogue:
                        if i in range(PE_X1, PE_X1 + 2 * TB, 2):
                            transpose_yd(b, c - 1, (i - PE_X1) // 2)
                        if i in range(PE_X2, PE_X2 + 2 * TB, 2):
                            transpose_x2(b, c - 1, (i - PE_X2) // 2)
                        if i == PE_LG:
                            logits(b)
                        if i == PE_RANK:
                            rank(b, c - 1)
                    if b.prologue:
                        if i in range(PE_U, PE_U + 2 * KB, 2):
                            transpose_xn(b, c + 1, (i - PE_U) // 2)
                        if i == PE_R:
                            project(b, 1 - b.par, "rank_dt", wx, P)
                        if i == PE_BC:
                            project(b, 1 - b.par, "bc", wbc, 64)
                        if i in range(PE_Z, PE_Z + 2 * KB, 2):
                            time_rank(b, (i - PE_Z) // 2)

            first = Body(-1, -1)
            for k in range(KB):
                transpose_xn(first, 0, k)
            project(first, 0, "rank_dt", wx, P)
            project(first, 0, "bc", wbc, 64)
            for k in range(KB):
                time_rank(first, k)
            for m in range(4):
                if m < 2:
                    spread_c(0, m, 0)
                spread_b(0, m, 0)
            bodies(pe, body)
            last = Body(NC, NC)
            for t in range(TB):
                transpose_yd(last, LAST, t)
            for t in range(TB):
                transpose_x2(last, LAST, t)
            logits(last)
            rank(last, LAST)
            wait(pe, "work_free", last.use("rank") + 1)
            nc.tensor.matmul(work[:, 0:E], ones[:], seen[:, TB], start=True, stop=True).then_inc(S["counts"], 1)

            def transpose_rows(j, q, loads):
                pe.wait_ge(tile_in[q], loads * 16)
                for k in range(KB):
                    last = nc.tensor.transpose(xT_ps[:, k * P:(k + 1) * P], xt[:, q, k * P:(k + 1) * P], ident[:])
                last.then_inc(S["xT_full"], 1)

            def transpose_act(j):
                pe.wait_ge(S["act_ready"], j + 1)
                for k in range(KB):
                    last = nc.tensor.transpose(aT_ps[:, k * P:(k + 1) * P], act[:, k * P:(k + 1) * P], ident[:])
                last.then_inc(S["aT_full"], 1)

            def weights_of(j):
                e_j = pe.value_load(t_exp[0:1, bass.ds(j, 1)], min_val=0, max_val=E - 1)
                return wexp[:, bass.ds(e_j % 2, 1)].rearrange("p a k w -> p (a k) w")

            def gate_up(j):
                w = weights_of(j)
                need = pe.value_load(t_need[0:1, bass.ds(j, 1)], min_val=16, max_val=16 * (TT + 1))
                pe.wait_ge(S["w_in"], need)
                pe.wait_ge(S["xT_ready"], j + 1)
                for half, dst in ((0, gate_ps), (1, up_ps)):
                    for k in range(KB):
                        last = nc.tensor.matmul(dst[:], xT[:, k, :], w[:, k, half * H:(half + 1) * H],
                                                start=k == 0, stop=k == KB - 1)
                last.then_inc(S["gu_full"], 1)

            def down(j):
                w = weights_of(j)
                pe.wait_ge(S["aT_ready"], j + 1)
                wait(pe, "y_ready", j)
                for k in range(KB):
                    last = nc.tensor.matmul(o_ps[:], aT[:, k, :], w[:, k, 2 * H:2 * H + DM], start=k == 0, stop=k == KB - 1)
                last.then_inc(S["o_full"], 1)

            pe.wait_ge(S["tables"], 1)
            transpose_rows(0, 0, 1)
            gate_up(0)
            transpose_rows(1, 1, 1)

            def turn_of_tiles(turn):
                for q in range(UN):
                    prev = turn * UN + q
                    transpose_act(prev)
                    gate_up(turn * UN + (q + 1))
                    transpose_rows(turn * UN + (q + 2), (q + 2) % UN, turn + ((q + 2) // UN + 1))
                    down(prev)

            turn_of_tiles(0)
            with pe.Fori(1, (TILES - UN) // UN) as turn:
                turn_of_tiles(turn)
            for j in range(TILES - UN + 1, TILES):
                transpose_act(j - 1)
                gate_up(j)
                if j + 1 < TILES:
                    transpose_rows(j + 1, (j + 1) % UN, (j + 1) // UN + 1)
                down(j - 1)
            transpose_act(TILES - 1)
            down(TILES - 1)


def kernel(L0_attn_x, L0_attn_A_log, L0_attn_D, L0_attn_x_proj_w, L0_attn_dt_proj_w, L0_attn_dt_proj_b,
           L0_ffn_router_logits, L0_ffn_gating_einsum, L0_ffn_linear, L0_ffn_per_expert_scale, L0_ffn_router_scale):
    import numpy as np
    import concourse.bacc as bacc
    from concourse.bass_utils import run_bass_kernel_spmd

    def columns(v):
        return np.asarray(v).reshape(-1, P).T

    x = np.asarray(L0_attn_x)
    B, T, DM = x.shape
    gating = np.asarray(L0_ffn_gating_einsum)
    down = np.asarray(L0_ffn_linear)
    E, _, H, F = gating.shape
    gate_up = gating.transpose(0, 3, 1, 2).reshape(E, F // P, P, 2 * H)
    weights = np.concatenate([gate_up, down.reshape(E, H // P, P, F)], axis=3).transpose(0, 2, 1, 3)
    arrays = {
        "x": x.reshape(B * T, DM),
        "A_log": L0_attn_A_log,
        "D": columns(L0_attn_D),
        "x_proj_T": np.asarray(L0_attn_x_proj_w).T,
        "dt_proj_T": np.asarray(L0_attn_dt_proj_w).T,
        "dt_bias": columns(L0_attn_dt_proj_b),
        "router_logits": L0_ffn_router_logits,
        "expert_weights": weights,
        "expert_scale": L0_ffn_per_expert_scale,
        "router_scale": columns(L0_ffn_router_scale),
    }
    arrays = {n: np.ascontiguousarray(a) for n, a in arrays.items()}
    nc = bacc.Bacc("TRN2", target_bir_lowering=False, num_devices=1)
    args = [nc.dram_tensor(n, a.shape, mybir.dt.from_np(a.dtype), kind="ExternalInput").ap() for n, a in arrays.items()]
    out = nc.dram_tensor("out", (B * T + P, DM), F32, kind="ExternalOutput").ap()
    selective_scan_moe_kernel(nc, *args, out)
    r = run_bass_kernel_spmd(nc, [arrays], core_ids=[0])
    return r.results[0]["out"][:B * T].reshape(B, T, DM)
```

```python
from contextlib import ExitStack

import concourse.bass as bass
from concourse import mybir

ALU = mybir.AluOpType
ACT = mybir.ActivationFunctionType
F32 = mybir.dt.float32
F32R = mybir.dt.float32r
I32 = mybir.dt.int32
U32 = mybir.dt.uint32
AX_X = mybir.AxisListType.X

P = 128
LN_EPS = 1e-5
RMS_EPS = 1e-6


def selective_scan_moe_kernel(nc, x, A_log, D, x_proj_T, dt_proj_T, dt_bias, router_logits,
                              expert_weights, expert_scale, router_scale, out):
    T, DM = x.shape
    NS = A_log.shape[1]
    R = dt_proj_T.shape[0]
    E = router_logits.shape[1]
    TOP_K = 2
    H = DM
    KB = DM // P
    CH = 512
    NC = T // CH
    TB = CH // P
    GB = 2
    NG = KB // GB
    UNITS = KB * NS
    UG = UNITS // NG

    REGION = T + P
    TAG = DM
    WCOL = DM + 1
    ROW = DM + 1 + E
    UN = 4
    TILES = -(-((TOP_K * T - E) // P + E) // UN) * UN
    TT = TILES + UN
    WROW = 2 * H + DM

    HR, PR, BR, DR = 4, 8, 8, 4
    NB = NG * NS
    BRR = 4

    ctx = ExitStack()
    with ctx:
        def sb(name, shape, dt=F32):
            return ctx.enter_context(nc.sbuf_tensor(name, shape, dt))

        def ps(name):
            return ctx.enter_context(nc.psum_tensor(name, [P, 512], F32))

        def sem(name):
            return ctx.enter_context(nc.semaphore(name))

        sorted_rows = nc.dram_tensor("sorted_rows", [E * REGION + P, ROW], F32).ap()

        ident = sb("ident", [P, P])
        before = sb("before", [P, P])
        ones = sb("ones", [P, P])
        pick = sb("pick", [64, 2 * NS, P], F32R)
        wx = sb("wx", [P, KB, R])
        wbc = sb("wbc", [P, KB, 64])
        wdt = sb("wdt", [P, DM])
        bdt = sb("bdt", [P, KB])
        a_neg = sb("a_neg", [P, KB, NS])
        d_skip = sb("d_skip", [P, KB])
        d_diag = sb("d_diag", [P, KB, P])
        rscale = sb("rscale", [P, KB])
        wr = sb("wr", [P, KB, E])
        escale = sb("escale", [P, E])
        iota_e = sb("iota_e", [P, E])
        region_of = sb("region_of", [P, E])
        pad_rows = sb("pad_rows", [P, ROW])
        pid = sb("pid", [P, 1])

        scanned = sb("scanned", [P, 3, 2, KB, CH])
        delta, du, u = scanned[:, 0], scanned[:, 1], scanned[:, 2]
        x_in = sb("x_in", [P, 2, TB, DM])
        bc = sb("bc", [64, 2, CH], F32R)
        xn = sb("xn", [P, TB, DM])
        dr = sb("dr", [P, CH])
        zabs = sb("zabs", [P, 2, CH])
        brep = sb("brep", [P, BRR, CH])
        dbu = sb("dbu", [P, BR, CH])
        da = sb("da", [P, DR, CH])
        h = sb("h", [P, HR, CH])
        prod = sb("prod", [P, PR, CH])
        state = sb("state", [P, UNITS])
        yd = sb("yd", [P, KB, CH])
        x1 = sb("x1", [P, TB, DM])
        rows = sb("rows", [P, TB, ROW])
        x2T = sb("x2T", [P, TB, KB, P])
        st6 = sb("st6", [P, 2, TB, 6])
        mv = sb("mv", [P, 2, TB, 2])
        var_eps = sb("var_eps", [P, 2, TB])
        rstd = sb("rstd", [P, 2, TB])
        nmr = sb("nmr", [P, 2, TB])
        neg_half = sb("neg_half", [P, TB])
        mean_sq = sb("mean_sq", [P, TB])
        rrms = sb("rrms", [P, TB])
        lg = sb("lg", [P, TB, E])
        mx = sb("mx", [P, TB, E])
        ix = sb("ix", [P, TB, E], U32)
        ixf = sb("ixf", [P, TB, TOP_K])
        ex = sb("ex", [P, TB, E])
        s1 = sb("s1", [P, TB])
        oh = sb("oh", [P, TOP_K, TB, E])
        chosen = sb("chosen", [P, TB, E])
        seen = sb("seen", [P, TB + 1, E])
        place = sb("place", [P, TB, E])
        slotf = sb("slotf", [P, TOP_K, TB])
        slot = sb("slot", [P, TOP_K, TB], I32)
        tagf = sb("tagf", [P, TB])

        cnt = sb("cnt", [P, E])
        padf = sb("padf", [P, E])
        pad_slot = sb("pad_slot", [P, E], I32)
        t_i = sb("t_i", [P, E], I32)
        nt = sb("nt", [P, E])
        incl = sb("incl", [P, E])
        excl = sb("excl", [P, E])
        zero_e = sb("zero_e", [P, E])
        jrow = sb("jrow", [1, TT])
        w3 = sb("w3", [1, TT, E])
        v3 = sb("v3", [1, TT, E])
        base_e = sb("base_e", [1, E])
        need_e = sb("need_e", [1, E])
        jt = sb("jt", [1, TT])
        t_row = sb("t_row", [1, TT], I32)
        t_exp = sb("t_exp", [1, TT], I32)
        t_load = sb("t_load", [1, TT], I32)
        t_need = sb("t_need", [1, TT], I32)
        e_f = sb("e_f", [1, TT])

        wexp = scanned[:].rearrange("p a b k c -> p (a b k c)").rearrange("p (s k w) -> p s k w", s=2, k=KB)
        xT = xn[:, 0].rearrange("p (k t) -> p k t", t=P)
        aT = xn[:, 1].rearrange("p (k t) -> p k t", t=P)
        act, g_act = xn[:, 2], xn[:, 3]
        xt = prod[:].rearrange("p r c -> p (r c)")[:, 0:UN * ROW].rearrange("p (q w) -> p q w", w=ROW)
        cw = sb("cw", [P, UN])
        tag = sb("tag", [P, UN], I32)
        ysb = x1[:, 0:2]

        bank = [ps(f"bank{i}") for i in range(8)]
        y_ps, c_ps, b_ps, work = bank[0:2], bank[2:4], bank[4:6], bank[6:8]
        xT_ps, gate_ps, up_ps, aT_ps, o_ps = bank[0], bank[1], bank[2], bank[3], bank[4]

        S = {n: sem(n) for n in (
            "waited_alone pads_placed var_ready var2_ready var_eps_ready var2_eps_ready rstd_ready rstd2_ready "
            "stats_ready stats2_ready mean_sq_ready rms_ready consts pick_ready "
            "weights_in a_exp a_ready diag_ready y_full wr_ready x_in_done xn_ready work_full work_free0 work_free1 "
            "bc_hi z_ready exp_z_ready softplus_ready delta_ready du_ready "
            "b_full b_copied c_full da_ready dbu_ready scan_done prod_ready prod_used state_saved y_taken "
            "x1_stored x2_ready ex_in ex_ready rows_ready slots_ready rows_out chosen_ready "
            "prologue_v epilogue_v tables_v counts tables pad_ready w_in xT_full xT_ready gu_full "
            "gelu_ready act_ready aT_full aT_ready o_full y_ready tag_ready added cw_ready").split()}
        tile_in = [sem(f"tile_in{q}") for q in range(UN)]

        block = ctx.enter_context(nc.Block())

        def alone(eng):
            eng.sem_inc(S["waited_alone"], 1)

        def wait(eng, name, count):
            if not isinstance(count, int) or count > 0:
                eng.wait_ge(S[name], count)

        class Chain:

            def __init__(self, eng, name, base=0):
                self.eng, self.name, self.base, self.k = eng, name, base, 0

            def did(self, ins):
                self.k += 1
                ins.then_inc(S[self.name], 1)

            def so_far(self):
                wait(self.eng, self.name, self.base + self.k)

            def link(self, ins):
                self.did(ins)
                self.so_far()

        LAST = NC - 1
        X1 = [("x1", t) for t in range(TB)]
        LATE_Z = [("z", k) for k in range(GB, KB)]
        X2 = [("x2", t) for t in range(TB)] + [("logits", 0)]
        U = [("u", k) for k in range(KB)]
        RANK = [("rank", 0)]
        NEXT = [("rank_dt", 0), ("bc", 0)] + [("z", k) for k in range(GB)]

        def work_use(c, what, k=0):
            epilogue, prologue, scan = c >= 1, c < LAST, 0 <= c < NC
            order = (X1 * epilogue + LATE_Z * scan + X2 * epilogue + U * prologue + RANK * epilogue
                     + NEXT * prologue)
            return order.index((what, k)) if what else len(order)

        IDENT, CONSTS = 2, 4
        USES = [work_use(c, None) for c in range(-1, NC + 1)]
        assert all(n % 2 == 0 for n in USES) and len(set(USES[2:-2])) == 1
        TURNS_MID = USES[2] // 2
        TURNS_0 = (USES[0] + USES[1]) // 2 - TURNS_MID

        class Body:

            def __init__(self, c, kind):
                self.c, self.kind, self.par = c, kind, kind % 2
                if kind <= 0:
                    self.turns = sum(USES[0:kind + 1]) // 2
                elif kind < NC:
                    self.turns = c * TURNS_MID + TURNS_0
                else:
                    self.turns = sum(USES[0:NC + 1]) // 2
                self.epilogue, self.prologue = kind >= 1, kind < LAST

            def use(self, what, k=0):
                return self.turns * 2 + work_use(self.kind, what, k)

            def work(self, what, k=0):
                return work[work_use(self.kind, what, k) % 2]

            def free(self, what, k=0):
                return S[f"work_free{work_use(self.kind, what, k) % 2}"]

            def wait_bank(self, eng, what, k=0, read=0):
                n = work_use(self.kind, what, k)
                wait(eng, f"work_free{n % 2}", self.turns + (n // 2 + read))

        def bodies(eng, run):
            run(Body(0, 0))
            with eng.Fori(0, (NC - 2) // 2) as pair:
                run(Body(pair * 2 + 1, 1))
                run(Body(pair * 2 + 2, 2))
            run(Body(LAST, LAST))

        def rows_sent(c):
            return 16 + c * (TB * TOP_K * 16)

        def x1_chunks(c):
            return 16 + c * 16

        ACT_Y = 4
        PE_X1, DVE_X1, DVE_ST2 = 3, 6, 7
        POOL_R2, DVE_N2, ACT_X2, POOL_RMS = 15, 16, 19, 22
        PE_X2, ACT_X2T, PE_LG = 18, 23, 25
        DVE_LG, ACT_EX, PE_RANK, DVE_PLACE, POOL_ROWS = 31, 36, 36, 37, 47
        DVE_ST1, POOL_R1, DVE_N1, ACT_XN = 15, 23, 24, 27
        PE_U, ACT_U, PE_R, ACT_R = 30, 35, 37, 48
        PE_BC, ACT_BC, DVE_BC = 44, 55, 55
        PE_Z, ACT_Z, DVE_Z = 52, 58, 59
        PE_LATE, ACT_LATE, DVE_LATE, POOL_LATE = 8, 15, 16, 27

        @block.sync
        def _(sp):
            def load_x(c, par):
                sp.dma_start(x_in[:, par], x[bass.ds(c * CH, CH), :].rearrange("(b p) d -> p b d", p=P))\
                  .then_inc(S["x_in_done"], 16)

            load_x(0, 0)
            n = 0
            for dst, src in (
                (wx[:], x_proj_T[:, 0:R].rearrange("(k p) e -> p k e", p=P)),
                (wbc[:, :, 0:32], x_proj_T[:, R:R + 2 * NS].rearrange("(k p) e -> p k e", p=P)),
                (wbc[:, :, 32:64], x_proj_T[:, R:R + 2 * NS].rearrange("(k p) e -> p k e", p=P)),
                (wdt[:], dt_proj_T),
                (bdt[:], dt_bias),
                (a_neg[:], A_log.rearrange("(k p) n -> p k n", p=P)),
                (d_skip[:], D),
                (rscale[:], router_scale),
                (wr[:], router_logits.rearrange("(k p) e -> p k e", p=P)),
                (escale[:], expert_scale.partition_broadcast(P)),
            ):
                sp.dma_start(dst, src).then_inc(S["weights_in"], 16)
                n += 1
            assert n == 10
            sp.wait_ge(S["consts"], CONSTS)
            sp.dma_start(out[T:T + P, :], pad_rows[:, 0:DM]).then_inc(S["x1_stored"], 16)

            def store_x1(c):
                sp.dma_start(out[bass.ds(c * CH, CH), :].rearrange("(b p) d -> p b d", p=P), x1[:])\
                  .then_inc(S["x1_stored"], 16)

            def body(b):
                if b.epilogue:
                    b.wait_bank(sp, "x1", TB - 2, read=1)
                    b.wait_bank(sp, "x1", TB - 1, read=1)
                    store_x1(b.c - 1)
                if b.prologue:
                    wait(sp, "x_in_done", (b.c + 1) * 16)
                    load_x(b.c + 1, 1 - b.par)

            bodies(sp, body)
            Body(NC, NC).wait_bank(sp, "x1", TB - 2, read=1)
            Body(NC, NC).wait_bank(sp, "x1", TB - 1, read=1)
            store_x1(LAST)
            wait(sp, "y_taken", NC * KB)
            sp.dma_start(wexp[:, 0], expert_weights[0]).then_inc(S["w_in"], 16)
            sp.wait_ge(S["tables"], 1)
            sp.wait_ge(S["rows_out"], rows_sent(NC))
            sp.wait_ge(S["pads_placed"], 16 * E)

            def load_tile(j, slot_):
                row = sp.value_load(t_row[0:1, bass.ds(j, 1)], min_val=0, max_val=E * REGION)
                sp.dma_start(xt[:, slot_], sorted_rows[bass.ds(row, P), :]).then_inc(tile_in[slot_], 16)

            def load_weights(j):
                sp.wait_ge(S["w_in"], j * 16 + 16)
                fresh = sp.value_load(t_load[0:1, bass.ds(j, 1)], min_val=0, max_val=E - 1)
                sp.dma_start(wexp[:, bass.ds(fresh % 2, 1)].rearrange("p a k w -> p (a k w)"),
                             expert_weights[bass.ds(fresh, 1)].rearrange("a p k w -> (a p) (k w)"),
                             cond=fresh > 0).then_inc(S["w_in"], 16)

            for q in range(UN):
                load_tile(q, q)

            def next_loads(j, q):
                wait(sp, "o_full", j)
                load_weights(j)
                sp.wait_ge(S["xT_full"], j + 1)
                sp.wait_ge(S["tag_ready"], j + 1)
                load_tile(j + UN, q)

            for q in range(UN):
                next_loads(q, q)
            with sp.Fori(1, TILES // UN) as turn:
                for q in range(UN):
                    next_loads(turn * UN + q, q)
            sp.wait_ge(S["w_in"], (TILES + 1) * 16)
            for q in range(UN):
                sp.wait_ge(tile_in[q], TT // UN * 16)

        @block.gpsimd
        def _(gp):
            def inverse_root(which, signal, done, ready, count):
                wait(gp, signal, count)
                alone(gp)
                gp.tensor_scalar(var_eps[:, which], mv[:, which, :, 1], LN_EPS, None, ALU.add).then_inc(S[done], 1)
                wait(gp, done, count)
                gp.tensor_tensor(rstd[:, which], var_eps[:, which], neg_half[:], ALU.pow).then_inc(S[ready], 1)

            def inverse_rms(c):
                own = Chain(gp, "mean_sq_ready", 3 * c)
                wait(gp, "rstd2_ready", c + 1)
                own.link(gp.tensor_tensor(mean_sq[:], rstd[:, 1], rstd[:, 1], ALU.mult))
                own.link(gp.tensor_tensor(mean_sq[:], mean_sq[:], mv[:, 1, :, 1], ALU.mult))
                alone(gp)
                own.link(gp.tensor_scalar(mean_sq[:], mean_sq[:], RMS_EPS, None, ALU.add))
                gp.tensor_tensor(rrms[:], mean_sq[:], neg_half[:], ALU.pow).then_inc(S["rms_ready"], 1)

            def send_rows(c, k):
                if k == 0:
                    wait(gp, "slots_ready", c + 1)
                    wait(gp, "rows_ready", c + 1)
                    alone(gp)
                gp.indirect_dma_start(out=sorted_rows,
                                      out_offset=bass.IndirectOffsetOnAxis(ap=slot[:, k % TOP_K, k // TOP_K:k // TOP_K + 1], axis=0),
                                      in_=rows[:, k // TOP_K, :], in_offset=None).then_inc(S["rows_out"], 16)

            def body(b):
                c = b.c
                for i in range(UNITS):
                    g, n, dd = i // UG, i % UG // GB, i % GB
                    q = g * GB + dd
                    if dd == 0:
                        wait(gp, "b_copied", c * NB + (g * NS + n + 1))
                    if n == 0:
                        wait(gp, "du_ready", c * KB + (q + 1))
                    wait(gp, "scan_done", c * UNITS + (i - BR + 1))
                    gp.tensor_tensor(dbu[:, i % BR],
                                     du[:, b.par, q], brep[:, (g * NS + n) % BRR], ALU.mult).then_inc(S["dbu_ready"], 1)
                    if i in range(POOL_LATE, POOL_LATE + 2 * (KB - GB), 2):
                        k = (i - POOL_LATE) // 2 + GB
                        wait(gp, "delta_ready", c * KB + (k + 1))
                        gp.tensor_tensor(du[:, b.par, k], delta[:, b.par, k], u[:, b.par, k], ALU.mult).then_inc(S["du_ready"], 1)
                    if b.epilogue and i == POOL_R2:
                        inverse_root(1, "var2_ready", "var2_eps_ready", "rstd2_ready", c)
                    if b.epilogue and i == POOL_RMS:
                        inverse_rms(c - 1)
                    if b.prologue and i == POOL_R1:
                        inverse_root(0, "var_ready", "var_eps_ready", "rstd_ready", c + 2)
                    if b.epilogue and i in range(POOL_ROWS, POOL_ROWS + 2 * TB * TOP_K, 2):
                        send_rows(c - 1, (i - POOL_ROWS) // 2)

            own = Chain(gp, "consts")
            gp.memset(neg_half[:], -0.5)
            own.link(gp.memset(ident[:], 0.0))
            own.link(gp.affine_select(out=ident[:], in_=ident[:], compare_op=ALU.not_equal, fill=1.0, base=0,
                                      pattern=[[-1, P]], channel_multiplier=1))
            assert own.k == IDENT
            inverse_root(0, "var_ready", "var_eps_ready", "rstd_ready", 1)
            gp.memset(before[:], 1.0)
            gp.memset(pad_rows[:], 0.0)
            gp.memset(zero_e[:], 0.0)
            gp.memset(state[:], 0.0)
            gp.memset(seen[:, TB, :], 0.0)
            own.link(gp.memset(ones[:], 1.0))
            gp.affine_select(out=before[:], in_=before[:], compare_op=ALU.is_gt, fill=0.0, base=0,
                             pattern=[[1, P]], channel_multiplier=-1)
            gp.iota(iota_e[:], pattern=[[1, E]], base=0, channel_multiplier=0, allow_small_or_imprecise_dtypes=True)
            gp.iota(region_of[:], pattern=[[REGION, E]], base=0, channel_multiplier=0, allow_small_or_imprecise_dtypes=True)
            gp.iota(pid[:], pattern=[[0, 1]], base=0, channel_multiplier=1, allow_small_or_imprecise_dtypes=True)
            gp.iota(tagf[:], pattern=[[P, TB]], base=0, channel_multiplier=1, allow_small_or_imprecise_dtypes=True)
            gp.iota(jrow[:], pattern=[[1, TT]], base=0, channel_multiplier=0, allow_small_or_imprecise_dtypes=True)
            own.link(gp.iota(pad_rows[:, TAG:TAG + 1].bitcast(I32), pattern=[[0, 1]], base=T, channel_multiplier=1))
            assert own.k == CONSTS
            gp.dma_start(sorted_rows[E * REGION:E * REGION + P, :], pad_rows[:]).then_inc(S["rows_out"], 16)
            bodies(gp, body)
            inverse_root(1, "var2_ready", "var2_eps_ready", "rstd2_ready", NC)
            inverse_rms(LAST)
            for k in range(TB * TOP_K):
                send_rows(LAST, k)
            gp.wait_ge(S["pad_ready"], 1)
            for e in range(E):
                gp.indirect_dma_start(out=sorted_rows, out_offset=bass.IndirectOffsetOnAxis(ap=pad_slot[:, e:e + 1], axis=0),
                                      in_=pad_rows[:], in_offset=None).then_inc(S["pads_placed"], 16)
            gp.wait_ge(S["x1_stored"], x1_chunks(NC))

            def add_tile(j, q):
                gp.wait_ge(S["tag_ready"], j + 1)
                gp.wait_ge(S["y_ready"], j + 1)
                wait(gp, "added", j * 16)
                alone(gp)
                gp.indirect_dma_start(out=out, out_offset=bass.IndirectOffsetOnAxis(ap=tag[:, q:q + 1], axis=0),
                                      in_=ysb[:, q % 2], in_offset=None, compute_op=ALU.add).then_inc(S["added"], 16)

            for q in range(UN):
                add_tile(q, q)
            with gp.Fori(1, TILES // UN) as turn:
                for q in range(UN):
                    add_tile(turn * UN + q, q)
            gp.wait_ge(S["added"], 16 * TILES)

        @block.scalar
        def _(ac):
            nc.scalar.preload_act_table_set("natural_log_exp_and_others")

            def norm_x(c, par, t, transposed):
                if t == 0:
                    wait(ac, "stats_ready", c + 1)
                    wait(ac, "work_full", transposed)
                nc.scalar.activation(xn[:, t], x_in[:, par, t], ACT.Identity, bias=nmr[:, 0, t:t + 1],
                                     scale=rstd[:, 0, t:t + 1]).then_inc(S["xn_ready"], 1)

            def take(b, what, k=0):
                wait(ac, "work_full", b.use(what, k) + 1)

            def copy_u(b, c, par, k):
                take(b, "u", k)
                if k == 0:
                    wait(ac, "y_taken", (c - 1) * KB)
                nc.scalar.copy(u[:, par, k], b.work("u", k)[:]).then_inc(b.free("u", k), 1)

            def copy_r(b):
                take(b, "rank_dt")
                nc.scalar.copy(dr[:], b.work("rank_dt")[:]).then_inc(b.free("rank_dt"), 1)

            def copy_bc(b, par):
                take(b, "bc")
                nc.scalar.copy(bc[:, par], b.work("bc")[0:64, :]).then_inc(S["bc_hi"], 1)

            def softplus_1(b, c, par, k):
                take(b, "z", k)
                wait(ac, "delta_ready", c * KB + (k - 1))
                if k == 0:
                    wait(ac, "da_ready", (c - 1) * UNITS)
                nc.scalar.activation(zabs[:, k % 2], b.work("z", k)[:], ACT.Abs, bias=bdt[:, k:k + 1]).then_inc(S["z_ready"], 1)
                nc.scalar.activation(delta[:, par, k], b.work("z", k)[:], ACT.Relu, bias=bdt[:, k:k + 1])\
                  .then_inc(b.free("z", k), 1)
                wait(ac, "z_ready", c * KB + (k + 1))
                nc.scalar.activation(zabs[:, k % 2], zabs[:, k % 2], ACT.Exp, scale=-1.0).then_inc(S["exp_z_ready"], 1)

            def softplus_2(c, k):
                wait(ac, "exp_z_ready", c * KB + (k + 1))
                nc.scalar.activation(zabs[:, k % 2], zabs[:, k % 2], ACT.Ln, bias=1.0).then_inc(S["softplus_ready"], 1)

            def copy_b(c, m):
                count = c * NB + m
                wait(ac, "b_full", count + 1)
                wait(ac, "dbu_ready", (count - (BRR - 1)) * GB)
                nc.scalar.copy(brep[:, m % BRR], b_ps[m % 2][:]).then_inc(S["b_copied"], 1)

            def save_states(c, k):
                wait(ac, "scan_done", c * UNITS + (2 * k + 2))
                nc.scalar.copy(state[:, 2 * k:2 * k + 2], h[:, 2 * k % HR:2 * k % HR + 2, CH - 1]).then_inc(S["state_saved"], 1)

            def take_y(c, q):
                wait(ac, "y_full", c * KB + (q + 1))
                nc.scalar.copy(yd[:, q], y_ps[q % GB][:]).then_inc(S["y_taken"], 1)

            def norm_x1(c, t):
                if t == 0:
                    wait(ac, "stats2_ready", c + 1)
                    wait(ac, "rows_out", rows_sent(c))
                nc.scalar.activation(rows[:, t, 0:DM], x1[:, t], ACT.Identity, bias=nmr[:, 1, t:t + 1],
                                     scale=rstd[:, 1, t:t + 1]).then_inc(S["x2_ready"], 1)

            def copy_x2T(b, t):
                take(b, "x2", t)
                nc.scalar.copy(x2T[:, t].rearrange("p k t -> p (k t)"), b.work("x2", t)[:]).then_inc(b.free("x2", t), 1)

            def exps(c):
                wait(ac, "ex_in", c + 1)
                nc.scalar.activation(ex[:], ex[:], ACT.Exp).then_inc(S["ex_ready"], 1)

            def body(b):
                c = b.c
                for i in range(UNITS):
                    g, n, dd = i // UG, i % UG // GB, i % GB
                    q = g * GB + dd
                    m = g * NS + n
                    if dd == 0 and (b.prologue or m + 1 < NB):
                        copy_b(c, m + 1)
                    if n == 0:
                        wait(ac, "delta_ready", c * KB + (q + 1))
                    wait(ac, "scan_done", c * UNITS + (i - DR + 1))
                    nc.scalar.activation(da[:, i % DR], delta[:, b.par, q], ACT.Exp,
                                         scale=a_neg[:, q, n:n + 1]).then_inc(S["da_ready"], 1)
                    if dd == 1 and i > 1:
                        save_states(c, i // 2 - 1)
                    if i % UG in range(ACT_Y, ACT_Y + GB):
                        if g > 0:
                            take_y(c, (g - 1) * GB + i % UG - ACT_Y)
                        elif b.kind >= 1:
                            take_y(c - 1, (NG - 1) * GB + i % UG - ACT_Y)
                    if i == 1 and b.kind >= 1:
                        save_states(c - 1, UNITS // 2 - 1)
                    if b.epilogue:
                        if i in range(ACT_X2, ACT_X2 + TB):
                            norm_x1(c - 1, i - ACT_X2)
                        if i in range(ACT_X2T, ACT_X2T + 2 * TB, 2):
                            copy_x2T(b, (i - ACT_X2T) // 2)
                        if i == ACT_EX:
                            exps(c - 1)
                    if b.prologue:
                        if i in range(ACT_XN, ACT_XN + TB):
                            norm_x(c + 1, 1 - b.par, i - ACT_XN, b.turns * 2)
                        if i in range(ACT_U, ACT_U + 2 * KB, 2):
                            copy_u(b, c + 1, 1 - b.par, (i - ACT_U) // 2)
                        if i == ACT_R:
                            copy_r(b)
                        if i == ACT_BC:
                            copy_bc(b, 1 - b.par)
                        if i in range(ACT_Z, ACT_Z + 2 * GB, 2):
                            softplus_1(b, c + 1, 1 - b.par, (i - ACT_Z) // 2)
                        if i in range(ACT_Z + 1, ACT_Z + 1 + 2 * GB, 2):
                            softplus_2(c + 1, (i - ACT_Z - 1) // 2)
                    if i in range(ACT_LATE, ACT_LATE + 2 * GB, 2):
                        softplus_1(b, c, b.par, (i - ACT_LATE) // 2 + GB)
                    if i in range(ACT_LATE + 1, ACT_LATE + 1 + 2 * GB, 2):
                        softplus_2(c, (i - ACT_LATE - 1) // 2 + GB)

            first = Body(-1, -1)
            for t in range(TB):
                norm_x(0, 0, t, 0)
            ac.wait_ge(S["weights_in"], 160)
            nc.scalar.activation(a_neg[:], a_neg[:], ACT.Exp).then_inc(S["a_exp"], 1)
            for k in range(KB):
                copy_u(first, 0, 0, k)
            copy_r(first)
            copy_bc(first, 0)
            for k in range(GB):
                softplus_1(first, 0, 0, k)
                softplus_2(0, k)
            copy_b(0, 0)
            ac.wait_ge(S["a_ready"], 1)
            bodies(ac, body)
            last = Body(NC, NC)
            for q in range(KB - GB, KB):
                take_y(LAST, q)
            for t in range(TB):
                norm_x1(LAST, t)
            for t in range(TB):
                copy_x2T(last, t)
            exps(LAST)

            def copy_xT(j):
                ac.wait_ge(S["xT_full"], j + 1)
                nc.scalar.copy(xT.rearrange("p k t -> p (k t)"), xT_ps[:]).then_inc(S["xT_ready"], 1)

            def gelu(j):
                ac.wait_ge(S["gu_full"], j + 1)
                nc.scalar.activation(g_act, gate_ps[:], ACT.Gelu_apprx_tanh).then_inc(S["gelu_ready"], 1)

            def copy_aT(j):
                ac.wait_ge(S["aT_full"], j + 1)
                nc.scalar.copy(aT.rearrange("p k t -> p (k t)"), aT_ps[:]).then_inc(S["aT_ready"], 1)

            def tile(j, prev):
                copy_aT(prev)
                gelu(j)

            copy_xT(0)
            gelu(0)
            copy_xT(1)
            with ac.Fori(0, (TILES - UN) // UN) as turn:
                for q in range(UN):
                    tile(turn * UN + (q + 1), turn * UN + q)
                    copy_xT(turn * UN + (q + 2))
            for j in range(TILES - UN + 1, TILES):
                tile(j, j - 1)
                if j + 1 < TILES:
                    copy_xT(j + 1)
            copy_aT(TILES - 1)

        @block.vector
        def _(dv):
            def take(b, what, k=0):
                wait(dv, "work_full", b.use(what, k) + 1)

            def stats(own, which, src, t):
                own.did(nc.vector.bn_stats(st6[:, which, t], src))

            def aggregate(own, which, t, signal):
                own.so_far()
                alone(dv)
                last = nc.vector.bn_aggr(mv[:, which, t], st6[:, which, t])
                if t == TB - 1:
                    last.then_inc(S[signal], 1)
                else:
                    own.did(last)

            def shift(which, signal, done, count):
                wait(dv, signal, count)
                nc.vector.scalar_tensor_tensor(nmr[:, which], mv[:, which, :, 0], -1.0, rstd[:, which], ALU.mult, ALU.mult)\
                  .then_inc(S[done], 1)

            def split_bc(b, c, par):
                wait(dv, "bc_hi", c + 1)
                nc.vector.tensor_tensor(bc[32:64, par], b.work("bc")[32:64, :], bc[32:64, par].bitcast(F32), ALU.subtract)\
                  .then_inc(b.free("bc"), 1)

            def time_step(c, par, k):
                wait(dv, "softplus_ready", c * KB + (k + 1))
                nc.vector.tensor_tensor(delta[:, par, k], delta[:, par, k], zabs[:, k % 2], ALU.add).then_inc(S["delta_ready"], 1)
                if k < GB:
                    wait(dv, "delta_ready", c * KB + (k + 1))
                    nc.vector.tensor_tensor(du[:, par, k], delta[:, par, k], u[:, par, k], ALU.mult).then_inc(S["du_ready"], 1)

            def scan(b, i):
                c = b.c
                wait(dv, "da_ready", c * UNITS + (i + 1))
                wait(dv, "dbu_ready", c * UNITS + (i + 1))
                if i % 2 == 0:
                    wait(dv, "state_saved", c * (UNITS // 2) + (i // 2 - 1))
                if i < HR:
                    wait(dv, "prod_ready", c * UNITS + (i - HR + 1))
                nc.vector.tensor_tensor_scan(h[:, i % HR], da[:, i % DR],
                                             dbu[:, i % BR],
                                             state[:, i:i + 1], ALU.mult, ALU.add).then_inc(S["scan_done"], 1)

            def times_c(b, i):
                c, g, n, dd = b.c, i // UG, i % UG // GB, i % GB
                if dd == 0:
                    wait(dv, "c_full", c * NB + (g * NS + n + 1))
                wait(dv, "scan_done", c * UNITS + (i + 1))
                wait(dv, "prod_used", c * UNITS + (i - PR + 1))
                nc.vector.tensor_tensor(prod[:, i % PR], h[:, i % HR], c_ps[n % 2][:], ALU.mult).then_inc(S["prod_ready"], 1)

            def residual(b, c, par, t):
                take(b, "x1", t)
                if t == 0:
                    wait(dv, "x1_stored", x1_chunks(c))
                nc.vector.tensor_tensor(x1[:, t], b.work("x1", t)[:], x_in[:, par, t], ALU.add).then_inc(b.free("x1", t), 1)

            def per_token(v):
                return v.unsqueeze(2).broadcast_to([P, TB, E])

            def route(b, c, own, k):
                V = nc.vector
                if k == 0:
                    wait(dv, "rms_ready", c + 1)
                    take(b, "logits")
                    V.tensor_tensor(lg[:], b.work("logits")[:, 0:TB * E].rearrange("p (b e) -> p b e", e=E), per_token(rrms[:]),
                                    ALU.mult).then_inc(b.free("logits"), 1)
                    return
                if k == 1:
                    b.wait_bank(dv, "logits", read=1)
                else:
                    own.so_far()
                if k == 1:
                    alone(dv)
                    for t in range(TB):
                        own.did(V.max(mx[:, t], lg[:, t]))
                elif k == 2:
                    alone(dv)
                    for t in range(TB):
                        own.did(V.max_index(ix[:, t], mx[:, t], lg[:, t]))
                elif k == 3:
                    V.tensor_tensor(ex[:], lg[:], mx[:, :, 0:1].broadcast_to([P, TB, E]), ALU.subtract).then_inc(S["ex_in"], 1)
                    own.did(V.tensor_copy(ixf[:], ix[:, :, 0:TOP_K]))
                elif k == 4:
                    for j in range(TOP_K):
                        own.did(V.tensor_tensor(oh[:, j], iota_e[:].unsqueeze(1).broadcast_to([P, TB, E]),
                                                ixf[:, :, j:j + 1].broadcast_to([P, TB, E]), ALU.is_equal))
                elif k == 5:
                    own.did(V.tensor_tensor(chosen[:], oh[:, 0], oh[:, 1], ALU.add))
                elif k == 6:
                    own.did(V.tensor_copy(seen[:, 0], seen[:, TB]))
                elif k <= 10:
                    t = k - 7
                    last = V.tensor_tensor(seen[:, t + 1], seen[:, t], chosen[:, t], ALU.add)
                    if t == TB - 1:
                        last.then_inc(S["chosen_ready"], 1)
                    else:
                        own.did(last)
                elif k == 11:
                    wait(dv, "ex_ready", c + 1)
                    own.did(V.tensor_reduce(s1[:], ex[:], axis=AX_X, op=ALU.add))
                elif k in (12, 16):
                    own.did(V.reciprocal(s1[:], s1[:]))
                elif k in (13, 17):
                    own.did(V.tensor_tensor(ex[:], ex[:], per_token(s1[:]), ALU.mult))
                elif k == 14:
                    own.did(V.tensor_tensor(ex[:], ex[:], chosen[:], ALU.mult))
                elif k == 15:
                    own.did(V.tensor_reduce(s1[:], ex[:], axis=AX_X, op=ALU.add))
                elif k == 18:
                    wait(dv, "rows_out", rows_sent(c))
                    own.did(V.tensor_tensor(rows[:, :, WCOL:WCOL + E], ex[:],
                                            escale[:].unsqueeze(1).broadcast_to([P, TB, E]), ALU.mult))
                elif k == 19:
                    own.did(V.tensor_copy(rows[:, :, TAG:TAG + 1].bitcast(I32), tagf[:].unsqueeze(2)))
                elif k == 20:
                    V.tensor_scalar(tagf[:], tagf[:], float(CH), None, ALU.add).then_inc(S["rows_ready"], 1)

            def places(b, c, own, k):
                V = nc.vector
                if k == 0:
                    take(b, "rank")
                    V.tensor_tensor(place[:], b.work("rank")[:, 0:TB * E].rearrange("p (b e) -> p b e", e=E),
                                    region_of[:].unsqueeze(1).broadcast_to([P, TB, E]), ALU.add).then_inc(b.free("rank"), 1)
                    return
                if k == 1:
                    b.wait_bank(dv, "rank", read=1)
                own.so_far()
                if k == 1:
                    for j in range(TOP_K):
                        own.did(V.tensor_tensor(oh[:, j], oh[:, j], place[:], ALU.mult))
                elif k == 2:
                    for j in range(TOP_K):
                        own.did(V.tensor_reduce(slotf[:, j], oh[:, j], axis=AX_X, op=ALU.add))
                elif k == 3:
                    V.tensor_copy(slot[:], slotf[:]).then_inc(S["slots_ready"], 1)

            STEPS = 21
            PER_P = 2 * TB - 1
            PER_E = 2 * TB - 1 + 29

            def body(b):
                c = b.c
                own_e = Chain(dv, "epilogue_v", (c - 1) * PER_E) if b.epilogue else None
                own_p = Chain(dv, "prologue_v", (c + 1) * PER_P) if b.prologue else None
                scan(b, 0)
                for i in range(UNITS):
                    g, n, dd = i // UG, i % UG // GB, i % GB
                    if i + 1 < UNITS:
                        scan(b, i + 1)
                    times_c(b, i)
                    if b.epilogue:
                        if i in range(DVE_X1, DVE_X1 + TB):
                            residual(b, c - 1, 1 - b.par, i - DVE_X1)
                        if i in range(DVE_ST2 + 1, DVE_ST2 + 1 + TB):
                            aggregate(own_e, 1, i - DVE_ST2 - 1, "var2_ready")
                        if i in range(DVE_ST2, DVE_ST2 + TB):
                            t = i - DVE_ST2
                            b.wait_bank(dv, "x1", t, read=1)
                            stats(own_e, 1, x1[:, t], t)
                        if i == DVE_N2:
                            shift(1, "rstd2_ready", "stats2_ready", c)
                        for k in range(3 * (i - DVE_LG), 3 * (i - DVE_LG + 1)):
                            if k in range(STEPS):
                                route(b, c - 1, own_e, k)
                        if i in range(DVE_PLACE, DVE_PLACE + 4):
                            places(b, c - 1, own_e, i - DVE_PLACE)
                    if b.prologue:
                        if i in range(DVE_ST1 + 1, DVE_ST1 + 1 + TB):
                            aggregate(own_p, 0, i - DVE_ST1 - 1, "var_ready")
                        if i in range(DVE_ST1, DVE_ST1 + TB):
                            if i == DVE_ST1:
                                wait(dv, "x_in_done", (c + 2) * 16)
                                wait(dv, "stats_ready", c + 1)
                            stats(own_p, 0, x_in[:, 1 - b.par, i - DVE_ST1], i - DVE_ST1)
                        if i == DVE_N1:
                            shift(0, "rstd_ready", "stats_ready", c + 2)
                        if i == DVE_BC:
                            split_bc(b, c + 1, 1 - b.par)
                        if i in range(DVE_Z, DVE_Z + 2 * GB, 2):
                            time_step(c + 1, 1 - b.par, (i - DVE_Z) // 2)
                    if i in range(DVE_LATE, DVE_LATE + 2 * GB, 2):
                        time_step(c, b.par, (i - DVE_LATE) // 2 + GB)
                assert own_p is None or own_p.k == PER_P, own_p.k
                assert own_e is None or own_e.k == PER_E, own_e.k

            own = Chain(dv, "prologue_v", 0)
            dv.wait_ge(S["x_in_done"], 16)
            for t in range(TB):
                stats(own, 0, x_in[:, 0, t], t)
            for t in range(TB):
                aggregate(own, 0, t, "var_ready")
            shift(0, "rstd_ready", "stats_ready", 1)
            dv.wait_ge(S["consts"], IDENT)
            nc.vector.tensor_tensor(pick[:], ident[0:64, 0:32].unsqueeze(2).broadcast_to([64, 2 * NS, P]),
                                    ident[0:64, 32:64].unsqueeze(2).broadcast_to([64, 2 * NS, P]), ALU.add)\
              .then_inc(S["pick_ready"], 1)
            dv.wait_ge(S["a_exp"], 1)
            nc.vector.tensor_scalar(a_neg[:], a_neg[:], -1.0, None, ALU.mult).then_inc(S["a_ready"], 1)
            for k in range(KB):
                nc.vector.tensor_scalar(d_diag[:, k], ident[:], d_skip[:, k:k + 1], None, ALU.mult).then_inc(S["diag_ready"], 1)
            for k in range(KB):
                nc.vector.tensor_scalar(wr[:, k], wr[:, k], rscale[:, k:k + 1], float(DM) ** -0.5, ALU.mult,
                                        ALU.mult).then_inc(S["wr_ready"], 1)
            split_bc(Body(-1, -1), 0, 0)
            for k in range(GB):
                time_step(0, 0, k)
            dv.wait_ge(S["consts"], CONSTS)
            bodies(dv, body)
            last = Body(NC, NC)
            own = Chain(dv, "epilogue_v", LAST * PER_E)
            for t in range(TB):
                residual(last, LAST, LAST % 2, t)
                last.wait_bank(dv, "x1", t, read=1)
                stats(own, 1, x1[:, t], t)
            for t in range(TB):
                aggregate(own, 1, t, "var2_ready")
            shift(1, "rstd2_ready", "stats2_ready", NC)
            for k in range(STEPS):
                route(last, LAST, own, k)
            for k in range(4):
                places(last, LAST, own, k)
            assert own.k == PER_E, own.k

            own = Chain(dv, "tables_v")
            dv.wait_ge(S["counts"], 1)
            own.link(nc.vector.tensor_copy(cnt[:], work[0][:, 0:E]))
            own.link(nc.vector.tensor_tensor(padf[:], cnt[:], region_of[:], ALU.add))
            own.link(nc.vector.tensor_scalar(padf[:], padf[:], pid[:], None, ALU.add))
            nc.vector.tensor_copy(pad_slot[:], padf[:]).then_inc(S["pad_ready"], 1)
            own.link(nc.vector.tensor_scalar(nt[:], cnt[:], float(P - 1), None, ALU.add))
            own.link(nc.vector.tensor_copy(t_i[:], nt[:]))
            own.link(nc.vector.tensor_scalar(t_i[:], t_i[:], P.bit_length() - 1, None, ALU.arith_shift_right))
            own.link(nc.vector.tensor_copy(nt[:], t_i[:]))
            own.link(nc.vector.tensor_scalar(nt[:], nt[:], 1.0, None, ALU.max))
            own.link(nc.vector.tensor_tensor_scan(incl[:], nt[:], zero_e[:], 0.0, ALU.add, ALU.add))
            own.link(nc.vector.tensor_tensor(excl[:], incl[:], nt[:], ALU.subtract))
            own.link(nc.vector.scalar_tensor_tensor(base_e[:], excl[0:1, :], float(-P), region_of[0:1, :], ALU.mult, ALU.add))
            own.link(nc.vector.memset(need_e[:], 16.0))
            own.link(nc.vector.tensor_scalar(need_e[:, 1:E], excl[0:1, 0:E - 1], 2.0, 16.0, ALU.add, ALU.mult))
            J = jrow[:].unsqueeze(2).broadcast_to([1, TT, E])

            def per_tile(v):
                return v.unsqueeze(1).broadcast_to([1, TT, E])

            own.link(nc.vector.tensor_tensor(w3[:], J, per_tile(incl[0:1, :]), ALU.is_ge))
            own.link(nc.vector.tensor_reduce(e_f[:], w3[:], axis=AX_X, op=ALU.add))
            own.link(nc.vector.tensor_scalar(jt[:], e_f[:], float(E - 1), None, ALU.min))
            own.link(nc.vector.tensor_copy(t_exp[:], jt[:]))
            own.link(nc.vector.tensor_tensor(w3[:], iota_e[0:1, :].unsqueeze(1).broadcast_to([1, TT, E]),
                                             e_f[:].unsqueeze(2).broadcast_to([1, TT, E]), ALU.is_equal))
            own.link(nc.vector.tensor_tensor(v3[:], w3[:], per_tile(need_e[:]), ALU.mult))
            own.link(nc.vector.tensor_reduce(jt[:], v3[:], axis=AX_X, op=ALU.add))
            own.link(nc.vector.tensor_scalar(jt[:], jt[:], 16.0, None, ALU.max))
            own.link(nc.vector.tensor_copy(t_need[:], jt[:]))
            own.link(nc.vector.tensor_scalar(v3[:], J, float(P), None, ALU.mult))
            own.link(nc.vector.tensor_tensor(v3[:], v3[:], per_tile(base_e[:]), ALU.add))
            own.link(nc.vector.tensor_tensor(v3[:], v3[:], w3[:], ALU.mult))
            own.link(nc.vector.tensor_reduce(jt[:], v3[:], axis=AX_X, op=ALU.add))
            own.link(nc.vector.tensor_scalar(e_f[:], e_f[:], float(E), float(E * REGION), ALU.is_equal, ALU.mult))
            own.link(nc.vector.tensor_tensor(jt[:], jt[:], e_f[:], ALU.add))
            own.link(nc.vector.tensor_copy(t_row[:], jt[:]))
            own.link(nc.vector.tensor_tensor(w3[:], J, per_tile(excl[0:1, :]), ALU.is_equal))
            own.link(nc.vector.tensor_scalar(v3[:], iota_e[0:1, :].unsqueeze(1).broadcast_to([1, TT, E]), 1.0, None, ALU.add))
            own.link(nc.vector.tensor_tensor(w3[:], w3[:], v3[:], ALU.mult))
            own.link(nc.vector.tensor_reduce(jt[:], w3[:], axis=AX_X, op=ALU.add))
            own.link(nc.vector.tensor_scalar(e_f[:], jt[:], float(E), None, ALU.is_lt))
            own.link(nc.vector.tensor_tensor(jt[:], jt[:], e_f[:], ALU.mult))
            nc.vector.tensor_copy(t_load[:], jt[:]).then_inc(S["tables"], 1)

            def tags(j, q, loads):
                e_j = dv.value_load(t_exp[0:1, bass.ds(j, 1)], min_val=0, max_val=E - 1)
                dv.wait_ge(tile_in[q], loads * 16)
                nc.vector.tensor_copy(cw[:, q:q + 1], xt[:, q, bass.ds(e_j + WCOL, 1)]).then_inc(S["cw_ready"], 1)
                nc.vector.tensor_copy(tag[:, q:q + 1], xt[:, q, TAG:TAG + 1].bitcast(I32)).then_inc(S["tag_ready"], 1)

            def gate(j):
                dv.wait_ge(S["gelu_ready"], j + 1)
                nc.vector.tensor_tensor(act, g_act, up_ps[:], ALU.mult).then_inc(S["act_ready"], 1)

            def weigh(j, q):
                dv.wait_ge(S["o_full"], j + 1)
                dv.wait_ge(S["cw_ready"], j + 1)
                if isinstance(j, int) and j < 2:
                    pass
                else:
                    dv.wait_ge(S["added"], j * 16 - 16)
                nc.vector.tensor_scalar(ysb[:, q % 2], o_ps[:], cw[:, q:q + 1], None, ALU.mult).then_inc(S["y_ready"], 1)

            tags(0, 0, 1)
            gate(0)
            tags(1, 1, 1)
            gate(1)
            weigh(0, 0)
            with dv.Fori(0, (TILES - UN) // UN) as turn:
                for q in range(UN):
                    j = turn * UN + (q + 2)
                    tags(j, (q + 2) % UN, turn + ((q + 2) // UN + 1))
                    gate(j)
                    weigh(turn * UN + (q + 1), (q + 1) % UN)
            for j in range(TILES - UN + 2, TILES):
                tags(j, j % UN, j // UN + 1)
                gate(j)
                weigh(j - 1, (j - 1) % UN)
            weigh(TILES - 1, (TILES - 1) % UN)

        @block.tensor
        def _(pe):
            pe.wait_ge(S["consts"], IDENT)

            def transpose_xn(b, c, k):
                if k == 0:
                    wait(pe, "xn_ready", c * TB + TB)
                b.wait_bank(pe, "u", k)
                for t in range(TB):
                    last = nc.tensor.transpose(b.work("u", k)[:, t * P:(t + 1) * P], xn[:, t, k * P:(k + 1) * P], ident[:])
                last.then_inc(S["work_full"], 1)

            def project(b, par, what, w, rows_, k):
                if k == 0:
                    b.wait_bank(pe, what)
                b.wait_bank(pe, "u", k, read=1)
                mm = nc.tensor.matmul(b.work(what)[0:rows_, :], w[:, k, :], u[:, par, k, :], start=k == 0, stop=k == KB - 1)
                if k == KB - 1:
                    mm.then_inc(S["work_full"], 1)

            def time_rank(b, k):
                b.wait_bank(pe, "z", k)
                if k == 0:
                    b.wait_bank(pe, "rank_dt", read=1)
                nc.tensor.matmul(b.work("z", k)[:], wdt[:, k * P:(k + 1) * P], dr[:], start=True, stop=True)\
                  .then_inc(S["work_full"], 1)

            def spread_b(c, m, par):
                wait(pe, "b_copied", c * NB + (m - 1))
                nc.tensor.matmul(b_ps[m % 2][:], pick[:, m % NS], bc[:, par], start=True, stop=True).then_inc(S["b_full"], 1)

            def spread_c(c, m, par):
                wait(pe, "prod_ready", (c * NB + (m - 1)) * GB)
                nc.tensor.matmul(c_ps[m % 2][:], pick[:, NS + m % NS], bc[:, par], start=True, stop=True)\
                  .then_inc(S["c_full"], 1)

            def transpose_yd(b, c, t):
                if t == 0:
                    wait(pe, "y_taken", c * KB + KB)
                b.wait_bank(pe, "x1", t)
                for k in range(KB):
                    last = nc.tensor.transpose(b.work("x1", t)[:, k * P:(k + 1) * P], yd[:, k, t * P:(t + 1) * P], ident[:])
                last.then_inc(S["work_full"], 1)

            def transpose_x2(b, c, t):
                wait(pe, "x2_ready", c * TB + (t + 1))
                b.wait_bank(pe, "x2", t)
                for k in range(KB):
                    last = nc.tensor.transpose(b.work("x2", t)[:, k * P:(k + 1) * P], rows[:, t, k * P:(k + 1) * P], ident[:])
                last.then_inc(S["work_full"], 1)

            def logits(b, t):
                if t == 0:
                    b.wait_bank(pe, "logits")
                b.wait_bank(pe, "x2", t, read=1)
                for k in range(KB):
                    last = nc.tensor.matmul(b.work("logits")[:, t * E:(t + 1) * E], x2T[:, t, k, :], wr[:, k, :],
                                            start=k == 0, stop=k == KB - 1)
                if t == TB - 1:
                    last.then_inc(S["work_full"], 1)

            def rank(b, c):
                b.wait_bank(pe, "rank")
                wait(pe, "chosen_ready", c + 1)
                nc.tensor.matmul(b.work("rank")[:, 0:TB * E], before[:], chosen[:].rearrange("p b e -> p (b e)"), start=True, stop=False)
                nc.tensor.matmul(b.work("rank")[:, 0:TB * E], ones[:], seen[:, 0:TB].rearrange("p b e -> p (b e)"), start=False,
                                 stop=True).then_inc(S["work_full"], 1)

            def body(b):
                c = b.c
                for i in range(UNITS):
                    g, n, dd = i // UG, i % UG // GB, i % GB
                    m = g * NS + n
                    spread, ahead = (spread_b, 4) if dd == 0 else (spread_c, 2)
                    if m + ahead < NB or b.prologue:
                        if m + ahead == NB and dd == 0:
                            b.wait_bank(pe, "bc", read=1)
                        spread(c, m + ahead, b.par if m + ahead < NB else 1 - b.par)
                    if n == 0:
                        wait(pe, "y_taken", c * KB + (g * GB + dd - 1))
                    wait(pe, "prod_ready", c * UNITS + (i + 1))
                    nc.tensor.matmul(y_ps[dd][:], ident[:], prod[:, i % PR], start=n == 0, stop=False)\
                      .then_inc(S["prod_used"], 1)
                    if n == NS - 1:
                        q = g * GB + dd
                        nc.tensor.matmul(y_ps[dd][:], d_diag[:, q], u[:, b.par, q], start=False, stop=True)\
                          .then_inc(S["y_full"], 1)
                    if b.epilogue:
                        if i in range(PE_X1, PE_X1 + TB):
                            transpose_yd(b, c - 1, i - PE_X1)
                        if i in range(PE_X2, PE_X2 + 2 * TB, 2):
                            transpose_x2(b, c - 1, (i - PE_X2) // 2)
                        if i in range(PE_LG, PE_LG + TB):
                            logits(b, i - PE_LG)
                        if i == PE_RANK:
                            rank(b, c - 1)
                    if b.prologue:
                        if i in range(PE_U, PE_U + 2 * KB, 2):
                            transpose_xn(b, c + 1, (i - PE_U) // 2)
                        for k in range(KB):
                            if i == PE_R + 2 * k - k // 2:
                                project(b, 1 - b.par, "rank_dt", wx, P, k)
                            if i == PE_BC + 2 * k - k // 3:
                                project(b, 1 - b.par, "bc", wbc, 64, k)
                        if i in range(PE_Z, PE_Z + 3 * GB, 3):
                            time_rank(b, (i - PE_Z) // 3)
                    if i in range(PE_LATE, PE_LATE + 3 * GB, 3):
                        time_rank(b, (i - PE_LATE) // 3 + GB)

            first = Body(-1, -1)
            for k in range(KB):
                transpose_xn(first, 0, k)
            pe.wait_ge(S["weights_in"], 160)
            for k in range(KB):
                project(first, 0, "rank_dt", wx, P, k)
            for k in range(KB):
                project(first, 0, "bc", wbc, 64, k)
            for k in range(GB):
                time_rank(first, k)
            first.wait_bank(pe, "bc", read=1)
            pe.wait_ge(S["pick_ready"], 1)
            for m in range(4):
                if m < 2:
                    spread_c(0, m, 0)
                spread_b(0, m, 0)
            pe.wait_ge(S["wr_ready"], KB)
            pe.wait_ge(S["diag_ready"], KB)
            pe.wait_ge(S["consts"], CONSTS)
            bodies(pe, body)
            last = Body(NC, NC)
            for t in range(TB):
                transpose_yd(last, LAST, t)
            for t in range(TB):
                transpose_x2(last, LAST, t)
            for t in range(TB):
                logits(last, t)
            rank(last, LAST)
            last.wait_bank(pe, "rank", read=1)
            last.wait_bank(pe, "logits", read=1)
            nc.tensor.matmul(work[0][:, 0:E], ones[:], seen[:, TB], start=True, stop=True).then_inc(S["counts"], 1)

            def transpose_rows(j, q, loads):
                pe.wait_ge(tile_in[q], loads * 16)
                for k in range(KB):
                    last = nc.tensor.transpose(xT_ps[:, k * P:(k + 1) * P], xt[:, q, k * P:(k + 1) * P], ident[:])
                last.then_inc(S["xT_full"], 1)

            def transpose_act(j):
                pe.wait_ge(S["act_ready"], j + 1)
                for k in range(KB):
                    last = nc.tensor.transpose(aT_ps[:, k * P:(k + 1) * P], act[:, k * P:(k + 1) * P], ident[:])
                last.then_inc(S["aT_full"], 1)

            def weights_of(j):
                e_j = pe.value_load(t_exp[0:1, bass.ds(j, 1)], min_val=0, max_val=E - 1)
                return wexp[:, bass.ds(e_j % 2, 1)].rearrange("p a k w -> p (a k) w")

            def gate_up(j):
                w = weights_of(j)
                need = pe.value_load(t_need[0:1, bass.ds(j, 1)], min_val=16, max_val=16 * (TT + 1))
                pe.wait_ge(S["w_in"], need)
                pe.wait_ge(S["xT_ready"], j + 1)
                for half, dst in ((0, gate_ps), (1, up_ps)):
                    for k in range(KB):
                        last = nc.tensor.matmul(dst[:], xT[:, k, :], w[:, k, half * H:(half + 1) * H],
                                                start=k == 0, stop=k == KB - 1)
                last.then_inc(S["gu_full"], 1)

            def down(j):
                w = weights_of(j)
                pe.wait_ge(S["aT_ready"], j + 1)
                wait(pe, "y_ready", j)
                for k in range(KB):
                    last = nc.tensor.matmul(o_ps[:], aT[:, k, :], w[:, k, 2 * H:2 * H + DM], start=k == 0, stop=k == KB - 1)
                last.then_inc(S["o_full"], 1)

            pe.wait_ge(S["tables"], 1)
            transpose_rows(0, 0, 1)
            gate_up(0)
            transpose_rows(1, 1, 1)

            def turn_of_tiles(turn):
                for q in range(UN):
                    prev = turn * UN + q
                    transpose_act(prev)
                    gate_up(turn * UN + (q + 1))
                    transpose_rows(turn * UN + (q + 2), (q + 2) % UN, turn + ((q + 2) // UN + 1))
                    down(prev)

            turn_of_tiles(0)
            with pe.Fori(1, (TILES - UN) // UN) as turn:
                turn_of_tiles(turn)
            for j in range(TILES - UN + 1, TILES):
                transpose_act(j - 1)
                gate_up(j)
                if j + 1 < TILES:
                    transpose_rows(j + 1, (j + 1) % UN, (j + 1) // UN + 1)
                down(j - 1)
            transpose_act(TILES - 1)
            down(TILES - 1)


def kernel(L0_attn_x, L0_attn_A_log, L0_attn_D, L0_attn_x_proj_w, L0_attn_dt_proj_w, L0_attn_dt_proj_b,
           L0_ffn_router_logits, L0_ffn_gating_einsum, L0_ffn_linear, L0_ffn_per_expert_scale, L0_ffn_router_scale):
    import numpy as np
    import concourse.bacc as bacc
    from concourse.bass_utils import run_bass_kernel_spmd

    def columns(v):
        return np.asarray(v).reshape(-1, P).T

    x = np.asarray(L0_attn_x)
    B, T, DM = x.shape
    gating = np.asarray(L0_ffn_gating_einsum)
    down = np.asarray(L0_ffn_linear)
    E, _, H, F = gating.shape
    gate_up = gating.transpose(0, 3, 1, 2).reshape(E, F // P, P, 2 * H)
    weights = np.concatenate([gate_up, down.reshape(E, H // P, P, F)], axis=3).transpose(0, 2, 1, 3)
    arrays = {
        "x": x.reshape(B * T, DM),
        "A_log": L0_attn_A_log,
        "D": columns(L0_attn_D),
        "x_proj_T": np.asarray(L0_attn_x_proj_w).T,
        "dt_proj_T": np.asarray(L0_attn_dt_proj_w).T,
        "dt_bias": columns(L0_attn_dt_proj_b),
        "router_logits": L0_ffn_router_logits,
        "expert_weights": weights,
        "expert_scale": L0_ffn_per_expert_scale,
        "router_scale": columns(L0_ffn_router_scale),
    }
    arrays = {n: np.ascontiguousarray(a) for n, a in arrays.items()}
    nc = bacc.Bacc("TRN2", target_bir_lowering=False, num_devices=1)
    args = [nc.dram_tensor(n, a.shape, mybir.dt.from_np(a.dtype), kind="ExternalInput").ap() for n, a in arrays.items()]
    out = nc.dram_tensor("out", (B * T + P, DM), F32, kind="ExternalOutput").ap()
    selective_scan_moe_kernel(nc, *args, out)
    r = run_bass_kernel_spmd(nc, [arrays], core_ids=[0])
    return r.results[0]["out"][:B * T].reshape(B, T, DM)
```
